# Optimizing a Trainium2 kernel written in Bass

```python
import numpy as np
import jax
import jax.numpy as jnp

def _softmax(x, axis=-1):
    return jax.nn.softmax(x, axis=axis)

def _gelu(x):
    return jax.nn.gelu(x, approximate=True)

def _silu(x):
    return jax.nn.silu(x)

def _sigmoid(x):
    return jax.nn.sigmoid(x)

def _layernorm(x, axis=-1, eps=1e-05):
    m = jnp.mean(x, axis=axis, keepdims=True)
    v = jnp.var(x, axis=axis, keepdims=True)
    return (x - m) / jnp.sqrt(v + eps)

def _scatter_add(tgt, idx, src, axis=0):
    return tgt.at[idx].add(src)

def _segment_sum(src, seg, n):
    return jax.ops.segment_sum(src, seg, n)
kernel_name = 'mk_seq_postln_d1_jaxref_r4_e8eba2'

def setup_inputs(seed: int=0):
    np.random.seed(seed)
    _w = jnp.asarray

    def _L0_attn_setup():
        import jax, jax.numpy as jnp
        import numpy as np
        B, N, D, BS = (2, 1024, 512, 64)

        def rms_norm(x):
            eps = jnp.asarray(jnp.finfo(x.dtype).eps, x.dtype)
            return x * jax.lax.rsqrt(jnp.mean(x * x, axis=-1, keepdims=True) + eps)

        def la_kernel(q, k, v, bs):
            b, n, d = q.shape
            T = n // bs
            qc = q.reshape(b, T, bs, d).transpose(1, 0, 2, 3)
            kc = k.reshape(b, T, bs, d).transpose(1, 0, 2, 3)
            vc = v.reshape(b, T, bs, d).transpose(1, 0, 2, 3)
            mask = jnp.tril(jnp.ones((bs, bs), q.dtype))

            def step(kv, qkv):
                qt, kt, vt = qkv
                s = jnp.einsum('bid,bjd->bij', qt, kt) * mask
                ot = jnp.einsum('bij,bjd->bid', s, vt) + jnp.einsum('bid,bde->bie', qt, kv)
                kv = kv + jnp.einsum('bjd,bje->bde', kt, vt)
                return (kv, ot)
            kv0 = jnp.zeros((b, d, d), q.dtype)
            _, o = jax.lax.scan(step, kv0, (qc, kc, vc))
            return o.transpose(1, 0, 2, 3).reshape(b, n, d)
        key = jax.random.key(seed)
        ks = jax.random.split(key, 6)
        scale = 0.02
        x = jax.random.normal(ks[0], (B, N, D), jnp.float32)
        Wq = jax.random.normal(ks[1], (D, D), jnp.float32) * scale
        Wk = jax.random.normal(ks[2], (D, D), jnp.float32) * scale
        Wv = jax.random.normal(ks[3], (D, D), jnp.float32) * scale
        Wg = jax.random.normal(ks[4], (D, D), jnp.float32) * scale
        Wp = jax.random.normal(ks[5], (D, D), jnp.float32) * scale
        return {'x': x, 'Wq': Wq, 'Wk': Wk, 'Wv': Wv, 'Wg': Wg, 'Wp': Wp}
    _L0_attn_in = _L0_attn_setup()

    def _L0_ffn_setup():
        import jax, jax.numpy as jnp
        import numpy as np
        D_MODEL = 512
        D_EXPERT = 2048
        EPS = 1e-08

        def ternary_quant(w):
            scale = jnp.mean(jnp.abs(w)) + EPS
            q = jnp.clip(jnp.round(w / scale), -1.0, 1.0) * scale
            return w + jax.lax.stop_gradient(q - w)
        key = jax.random.key(seed)
        k_x, k_up, k_gate, k_down = jax.random.split(key, 4)
        std_in = 1.0 / np.sqrt(D_MODEL)
        std_exp = 1.0 / np.sqrt(D_EXPERT)
        return {'x': jax.random.normal(k_x, (4, 512, D_MODEL), dtype=jnp.float32), 'W_up': jax.random.normal(k_up, (D_EXPERT, D_MODEL), dtype=jnp.float32) * std_in, 'W_gate': jax.random.normal(k_gate, (D_EXPERT, D_MODEL), dtype=jnp.float32) * std_in, 'W_down': jax.random.normal(k_down, (D_MODEL, D_EXPERT), dtype=jnp.float32) * std_exp}
    _L0_ffn_in = _L0_ffn_setup()
    _d = {'L0_attn_x': _L0_attn_in['x'], 'L0_attn_Wq': _L0_attn_in['Wq'], 'L0_attn_Wk': _L0_attn_in['Wk'], 'L0_attn_Wv': _L0_attn_in['Wv'], 'L0_attn_Wg': _L0_attn_in['Wg'], 'L0_attn_Wp': _L0_attn_in['Wp'], 'L0_ffn_W_up': _L0_ffn_in['W_up'], 'L0_ffn_W_gate': _L0_ffn_in['W_gate'], 'L0_ffn_W_down': _L0_ffn_in['W_down']}
    _x0 = _d['L0_attn_x']
    _d['L0_attn_x'] = jax.random.normal(jax.random.fold_in(jax.random.key(seed), 1), (1, 4096, 512), dtype=_x0.dtype)
    del _x0
    return _d

def reference(L0_attn_x, L0_attn_Wq, L0_attn_Wk, L0_attn_Wv, L0_attn_Wg, L0_attn_Wp, L0_ffn_W_up, L0_ffn_W_gate, L0_ffn_W_down):

    def _L0_attn_ref(x, Wq, Wk, Wv, Wg, Wp):
        import jax, jax.numpy as jnp
        import numpy as np
        B, N, D, BS = (2, 1024, 512, 64)

        def rms_norm(x):
            eps = jnp.asarray(jnp.finfo(x.dtype).eps, x.dtype)
            return x * jax.lax.rsqrt(jnp.mean(x * x, axis=-1, keepdims=True) + eps)

        def la_kernel(q, k, v, bs):
            b, n, d = q.shape
            T = n // bs
            qc = q.reshape(b, T, bs, d).transpose(1, 0, 2, 3)
            kc = k.reshape(b, T, bs, d).transpose(1, 0, 2, 3)
            vc = v.reshape(b, T, bs, d).transpose(1, 0, 2, 3)
            mask = jnp.tril(jnp.ones((bs, bs), q.dtype))

            def step(kv, qkv):
                qt, kt, vt = qkv
                s = jnp.einsum('bid,bjd->bij', qt, kt) * mask
                ot = jnp.einsum('bij,bjd->bid', s, vt) + jnp.einsum('bid,bde->bie', qt, kv)
                kv = kv + jnp.einsum('bjd,bje->bde', kt, vt)
                return (kv, ot)
            kv0 = jnp.zeros((b, d, d), q.dtype)
            _, o = jax.lax.scan(step, kv0, (qc, kc, vc))
            return o.transpose(1, 0, 2, 3).reshape(b, n, d)
        xn = rms_norm(x)
        q = jax.nn.silu(jnp.einsum('bnd,od->bno', xn, Wq))
        k = jax.nn.silu(jnp.einsum('bnd,od->bno', xn, Wk))
        v = jax.nn.silu(jnp.einsum('bnd,od->bno', xn, Wv))
        g = jax.nn.sigmoid(jnp.einsum('bnd,od->bno', xn, Wg))
        o = la_kernel(q, k, v, BS) * g
        return jnp.einsum('bnd,od->bno', o, Wp)

    def _L0_ffn_ref(x, W_up, W_gate, W_down):
        import jax, jax.numpy as jnp
        import numpy as np
        D_MODEL = 512
        D_EXPERT = 2048
        EPS = 1e-08

        def ternary_quant(w):
            scale = jnp.mean(jnp.abs(w)) + EPS
            q = jnp.clip(jnp.round(w / scale), -1.0, 1.0) * scale
            return w + jax.lax.stop_gradient(q - w)
        wu = ternary_quant(W_up)
        wg = ternary_quant(W_gate)
        wd = ternary_quant(W_down)
        up = jnp.einsum('bsd,ed->bse', x, wu)
        gate = jnp.einsum('bsd,ed->bse', x, wg)
        hidden = jax.nn.silu(up) * gate
        return jnp.einsum('bse,de->bsd', hidden, wd)
    x = L0_attn_x
    x = _layernorm(x + _L0_attn_ref(x, L0_attn_Wq, L0_attn_Wk, L0_attn_Wv, L0_attn_Wg, L0_attn_Wp), axis=-1)
    x = _layernorm(x + _L0_ffn_ref(x, L0_ffn_W_up, L0_ffn_W_gate, L0_ffn_W_down), axis=-1)
    return x

_drawn_inputs = setup_inputs


def setup_inputs(seed=0):
    import zlib

    import numpy as np

    out = dict(_drawn_inputs(seed))
    spreads = {}
    factors = {}
    for name, (base, spread) in spreads.items():
        noise = np.random.default_rng([zlib.crc32(name.encode()), seed]).standard_normal(out[name].shape)
        drawn = base * np.exp(spread * noise) if base else spread * noise
        out[name] = jnp.asarray(drawn.astype(out[name].dtype))
    for name, factor in factors.items():
        out[name] = (out[name] * factor).astype(out[name].dtype)
    return out
```

```python
from contextlib import ExitStack

import numpy as np

import concourse.bass as bass
import concourse.mybir as mybir
from concourse.alu_op_type import AluOpType as ALU

ACT = mybir.ActivationFunctionType
AX = mybir.AxisListType
F32 = mybir.dt.float32
F32R = mybir.dt.float32r
F16 = mybir.dt.float16
I32 = mybir.dt.int32

P = 128
TOKENS, D, E = 4096, 512, 2048
KT = D // P
ET = E // P
CHUNKS = TOKENS // P
UNROLL = 4
BLOCK = 512
BLOCKS = TOKENS // BLOCK
TT = BLOCK // P

PIECE = 1024
MATS = 3
PIECES = MATS * D * E // (P * PIECE)
PER_MAT = PIECES // MATS
PER_STEP = PIECES // UNROLL

ROW_SCALE = 64.0
W_SCALE = 256.0
H_SCALE = 8.0
RMS_EPS = float(np.finfo(np.float32).eps)
LN_EPS = 1e-5
QUANT_EPS = 1e-8
EXPONENT_BITS = 0x7F800000
K_, Q_, G_, V_ = range(4)


def at(i, p):
    i = i + p // UNROLL
    p = p % UNROLL
    return i * UNROLL + p, i * 2 + p // 2, i, p


def build(nc, x, w_attn, w_ffn, out):
    ctx = ExitStack()
    phase_a = ExitStack()

    def sem(name):
        return ctx.enter_context(nc.semaphore(name))

    def sb(name, shape, dt, where=ctx):
        return where.enter_context(nc.sbuf_tensor(name, shape, dt))

    y_dram = nc.dram_tensor("y_dram", (CHUNKS, P, D), F32, kind="Internal").ap()
    yh_dram = nc.dram_tensor("yh_dram", (CHUNKS, P, D), F16, kind="Internal").ap()
    yl_dram = nc.dram_tensor("yl_dram", (CHUNKS, P, D), F16, kind="Internal").ap()

    codes = sb("codes", [P, MATS * ET, D], F16)
    yT = [sb(f"yT{b}", [P, 2, KT, BLOCK], F16) for b in range(2)]
    ffn_scale = sb("ffn_scale", [P, 16], F32)
    asum = sb("asum", [P, PIECES], F32)
    thr = sb("thr", [P, PIECES], F32)
    nthr = sb("nthr", [P, PIECES], F32)
    minus_half = sb("minus_half", [P, PER_MAT], F32)
    ln = sb("ln", [P, 2, 2], F32)
    stats = sb("stats", [P, 6], F32)
    rstd = sb("rstd", [P, 2], F32)
    ln2 = sb("ln2", [P, TT, 2], F32)
    stats2 = sb("stats2", [P, TT, 6], F32)
    rstd2 = sb("rstd2", [P, TT], F32)

    w_proj = sb("w_proj", [P, 4, 2, KT, D], F16, phase_a)
    w_out = [sb(f"w_out_{n}", [P, KT, D], F32R, phase_a) for n in ("hi", "lo")]
    stage = sb("stage", [P, 4, PIECE], F32, phase_a)
    below = sb("below", [P, PIECE], F16, phase_a)
    kv = [sb(f"kv_{n}", [P, KT, D], F32R, phase_a) for n in ("hi", "lo")]
    x32 = sb("x32", [P, UNROLL, D], F32, phase_a)
    xn = sb("xn", [P, 2, D], F16, phase_a)
    xnT = sb("xnT", [P, 2, 2, KT, P], F16, phase_a)
    q32 = sb("q32", [P, D], F32, phase_a)
    k32 = sb("k32", [P, D], F32, phase_a)
    v32 = sb("v32", [P, D], F32, phase_a)
    qT = [sb(f"qT_{n}", [P, KT, P], F32R, phase_a) for n in ("hi", "lo")]
    kT = [sb(f"kT_{n}", [P, KT, P], F32R, phase_a) for n in ("hi", "lo")]
    kN = [sb(f"kN_{n}", [P, D], F32R, phase_a) for n in ("hi", "lo")]
    vN = [sb(f"vN_{n}", [P, D], F32R, phase_a) for n in ("hi", "lo")]
    sT32 = sb("sT32", [P, P], F32, phase_a)
    sT = [sb(f"sT_{n}", [P, P], F32R, phase_a) for n in ("hi", "lo")]
    gate_t = sb("gate_t", [P, D], F32, phase_a)
    og32 = sb("og32", [P, D], F32, phase_a)
    ogT = [sb(f"ogT_{n}", [P, KT, P], F32R, phase_a) for n in ("hi", "lo")]
    u32 = sb("u32", [P, D], F32, phase_a)
    y32 = sb("y32", [P, D], F32, phase_a)
    yhl = sb("yhl", [P, 2, D], F16, phase_a)
    squares = sb("squares", [P, D], F16, phase_a)
    junk = sb("junk", [P, PIECE], F16, phase_a)
    causal = sb("causal", [P, P], F32, phase_a)
    ident = sb("ident", [P, P], F32, phase_a)
    wmax = sb("wmax", [P, 4], F32, phase_a)
    wmax_all = sb("wmax_all", [P, 4], F32, phase_a)
    wpow = sb("wpow", [P, 4], F32, phase_a)
    winv = sb("winv", [P, 4], F32, phase_a)
    wscale = sb("wscale", [P, 4], F32, phase_a)
    wunscale = sb("wunscale", [P, 4], F32, phase_a)
    msum = sb("msum", [P, 4], F32, phase_a)
    msum_all = sb("msum_all", [P, 4], F32, phase_a)
    ssq = sb("ssq", [P, 2], F32, phase_a)
    rms = sb("rms", [P, 2], F32, phase_a)
    phase_a.close()

    res = [sb(f"res{b}", [P, TT, D], F32) for b in range(2)]
    silu_u = sb("silu_u", [P, 2, BLOCK], F32)
    h32 = sb("h32", [P, BLOCK], F32)
    hT = [sb(f"hT_{n}", [P, 2, BLOCK], F16) for n in ("hi", "lo")]

    state = [ctx.enter_context(nc.psum_tensor(f"state{t}", [P, D], F32)) for t in range(4)]
    work = [ctx.enter_context(nc.psum_tensor(f"work{t}", [P, D], F32)) for t in range(4)]

    USES = 10
    TQ, TK, PK, SC, PQ, OO, TOG, PG, WP, PV = range(USES)

    def bank(p, use):
        return work[(USES * p + use) % 4]

    consts_ready = sem("consts_ready")
    passed = sem("passed")
    fill_done = sem("fill_done")
    w_loaded = [sem(f"w_loaded{s}") for s in range(2)]
    wmax_ready, wmax_all_ready = sem("wmax_ready"), sem("wmax_all_ready")
    small = sem("small")
    whi_ready, wlo_ready = sem("whi_ready"), sem("wlo_ready")
    piece_loaded = [sem(f"piece_loaded{s}") for s in range(4)]
    abs_done, msum_ready, msum_all_ready, thr_ready = (sem(n) for n in ("abs_done", "msum_ready", "msum_all_ready", "thr_ready"))
    below_ready, piece_coded = sem("below_ready"), sem("piece_coded")
    x_loaded = [sem(f"x_loaded{s}") for s in range(UNROLL)]
    ssq_ready, ms_ready, rms_ready = sem("ssq_ready"), sem("ms_ready"), sem("rms_ready")
    xhi_ready, xlo_ready = sem("xhi_ready"), sem("xlo_ready")
    xT_loaded = [sem(f"xT_loaded{s}") for s in range(2)]
    pk_done, pq_done, pg_done, pv_done = (sem(n) for n in ("pk_done", "pq_done", "pg_done", "pv_done"))
    k_ready, q_ready, g_ready, v_ready = (sem(n) for n in ("k_ready", "q_ready", "g_ready", "v_ready"))
    tq_done, tk_done, tog_done = (sem(n) for n in ("tq_done", "tk_done", "tog_done"))
    qThi_ready, qTlo_ready = sem("qThi_ready"), sem("qTlo_ready")
    kThi_ready, kTlo_ready = sem("kThi_ready"), sem("kTlo_ready")
    ogThi_ready, ogTlo_ready = sem("ogThi_ready"), sem("ogTlo_ready")
    kNhi_ready, kNlo_ready = sem("kNhi_ready"), sem("kNlo_ready")
    vNhi_ready, vNlo_ready = sem("vNhi_ready"), sem("vNlo_ready")
    s_done, s_masked, shi_ready, slo_ready = (sem(n) for n in ("s_done", "s_masked", "shi_ready", "slo_ready"))
    o_done, og_ready = sem("o_done"), sem("og_ready")
    state_done, kvhi_ready, kvlo_ready = sem("state_done"), sem("kvhi_ready"), sem("kvlo_ready")
    wp_done, u_ready = sem("wp_done"), sem("u_ready")
    stats_ready, mv_ready, vareps_ready, rstd_ready = (sem(n) for n in ("stats_ready", "mv_ready", "vareps_ready", "rstd_ready"))
    y_ready, yhi_ready, ylo_ready = sem("y_ready"), sem("yhi_ready"), sem("ylo_ready")
    y_stored = sem("y_stored")
    yT_loaded = [sem(f"yT_loaded{b}") for b in range(2)]
    res_loaded = [sem(f"res_loaded{b}") for b in range(2)]
    up_done, gate_done, down_done = sem("up_done"), sem("gate_done"), sem("down_done")
    silu_ready, h_ready, hhi_ready, hlo_ready = (sem(n) for n in ("silu_ready", "h_ready", "hhi_ready", "hlo_ready"))
    z_read, stats2_ready, mv2_ready, vareps2_ready, rstd2_ready = (
        sem(n) for n in ("z_read", "stats2_ready", "mv2_ready", "vareps2_ready", "rstd2_ready"))
    out_ready = sem("out_ready")
    out_stored = [sem(f"out_stored{b}") for b in range(2)]

    block = ctx.enter_context(nc.Block())

    def carry(engine):
        engine.sem_inc(passed, 1)

    @block.sync
    def _(sp):
        def load_weight(n):
            if n >= 2:
                sp.wait_ge(wlo_ready, n - 1)
            sp.dma_start(stage[:, 2 * (n % 2):2 * (n % 2) + 2, :], w_attn[n]).then_inc(w_loaded[n % 2], 16)

        def load_x(i, p):
            c, _, _, slot = at(i, p)
            sp.dma_start(x32[:, slot, :], x[c]).then_inc(x_loaded[slot], 16)

        def load_piece(t, slot):
            sp.dma_start(stage[:, slot, :], w_ffn[t]).then_inc(piece_loaded[slot], 16)

        def transpose_x(i, p):
            c, _, _, slot = at(i, p)
            sp.wait_ge(xhi_ready, c + 1)
            carry(sp)
            sp.dma_start(xnT[:, slot % 2, 0], xn[:, 0, :], transpose=True).then_inc(xT_loaded[slot % 2], 16)
            sp.wait_ge(xlo_ready, c + 1)
            carry(sp)
            sp.dma_start(xnT[:, slot % 2, 1], xn[:, 1, :], transpose=True).then_inc(xT_loaded[slot % 2], 16)

        def store_y(i, p):
            c, _, _, _ = at(i, p)
            sp.wait_ge(y_ready, c + 1)
            carry(sp)
            sp.dma_start(y_dram[c], y32[:]).then_inc(y_stored, 16)
            sp.wait_ge(yhi_ready, c + 1)
            carry(sp)
            sp.dma_start(yh_dram[c], yhl[:, 0, :]).then_inc(y_stored, 16)
            sp.wait_ge(ylo_ready, c + 1)
            carry(sp)
            sp.dma_start(yl_dram[c], yhl[:, 1, :]).then_inc(y_stored, 16)

        def step(i, p, first=False, summing=False, coding=False, last=False):
            c, _, _, _ = at(i, p)
            if coding:
                if p == 0:
                    sp.wait_ge(abs_done, PIECES)
                sp.wait_ge(piece_coded, c - UNROLL + 1)
                carry(sp)
                load_piece(c - UNROLL, p)
            if not first:
                store_y(i, p - 1)
            if summing:
                for t in range(PER_STEP * p, PER_STEP * (p + 1)):
                    if t >= 4:
                        sp.wait_ge(abs_done, t - 3)
                    load_piece(t, t % 4)
            if not (last and p >= 2):
                sp.wait_ge(pv_done, c + 1)
                carry(sp)
                transpose_x(i, p + 2)
            if not last:
                sp.wait_ge(u_ready, c + 1)
                carry(sp)
                load_x(i, p + UNROLL)

        load_x(0, 0)
        load_weight(K_)
        load_x(0, 1)
        load_weight(Q_)
        load_x(0, 2)
        load_x(0, 3)
        transpose_x(0, 0)
        load_weight(G_)
        load_weight(V_)
        sp.wait_ge(xT_loaded[0], 32)
        transpose_x(0, 1)
        load_weight(4)
        sp.wait_ge(wlo_ready, 5)
        for p in range(UNROLL):
            step(0, p, first=p == 0, summing=True)
        with sp.Fori(1, CHUNKS // UNROLL - 1) as i:
            for p in range(UNROLL):
                step(i, p, coding=True)
        for p in range(UNROLL):
            step(CHUNKS // UNROLL - 1, p, last=True)
        store_y(CHUNKS // UNROLL - 1, UNROLL - 1)

        def load_block(b, slot):
            rows = slice(None)
            for part, src in enumerate((yh_dram, yl_dram)):
                sp.dma_start(yT[slot][:, part], src[bass.ts(b, TT)].rearrange("t p d -> (t p) d"),
                             transpose=True).then_inc(yT_loaded[slot], 16)
            sp.dma_start(res[slot][:], y_dram[bass.ts(b, TT)].rearrange("t p d -> p t d")).then_inc(res_loaded[slot], 16)

        def store_block(b, slot):
            sp.wait_ge(out_ready, b + 1)
            carry(sp)
            sp.dma_start(out[bass.ts(b, TT)].rearrange("t p d -> p t d"), res[slot][:]).then_inc(out_stored[slot], 16)

        sp.wait_ge(y_stored, 48 * CHUNKS)
        load_block(0, 0)
        load_block(1, 1)
        with sp.Fori(0, BLOCKS // 2 - 1) as i:
            for s in range(2):
                b = i * 2 + s
                store_block(b, s)
                sp.wait_ge(out_stored[s], 16 * (i + 1))
                carry(sp)
                load_block(b + 2, s)
        for s in range(2):
            store_block(BLOCKS - 2 + s, s)
        for s in range(2):
            sp.wait_ge(out_stored[s], 16 * (BLOCKS // 2))

    @block.tensor
    def _(pe):
        def project(i, p, which, use, done):
            _, _, _, slot = at(i, p)
            dst = bank(p - 1, use)
            terms = ((0, 0), (0, 1), (1, 0))
            for n, (a, b) in enumerate(terms):
                for k in range(KT):
                    mm = pe.matmul(dst[:], xnT[:, slot % 2, a, k, :], w_proj[:, which, b, k, :],
                                   start=n == 0 and k == 0, stop=n == 2 and k == KT - 1)
            mm.then_inc(done, 1)

        def transposes(dst, src, done):
            for k in range(KT):
                mm = pe.transpose(dst[:, k * P:(k + 1) * P], src[:, k * P:(k + 1) * P], ident[:])
            mm.then_inc(done, 1)

        def split_product(dst, lhs, rhs, start, stop, slices):
            for n, (a, b) in enumerate(((0, 0), (0, 1), (1, 0))):
                for m, (sl, sr) in enumerate(slices):
                    mm = pe.matmul(dst, sl(lhs[a]), sr(rhs[b]),
                                   start=start and n == 0 and m == 0,
                                   stop=stop and n == 2 and m == len(slices) - 1, skip_group_check=True)
            return mm

        def step(i, p, first=False, last=False):
            c, _, _, _ = at(i, p)
            nxt = not (last and p == UNROLL - 1)
            pe.wait_ge(q_ready, c + 1)
            if first:
                pe.wait_ge(k_ready, 1)
            else:
                pe.wait_ge(ogTlo_ready, c)
            transposes(bank(p, TQ), q32, tq_done)
            pe.wait_ge(k_ready, c + 1)
            pe.wait_ge(g_ready, c + 1)
            transposes(bank(p, TK), k32, tk_done)
            if not first:
                pe.wait_ge(u_ready, c)
            if nxt:
                _, c2, _, slot = at(i, p + 1)
                pe.wait_ge(xT_loaded[slot % 2], 32 * (c2 + 1))
                project(i, p + 1, K_, PK, pk_done)
            pe.wait_ge(qTlo_ready, c + 1)
            pe.wait_ge(kTlo_ready, c + 1)
            pe.wait_ge(v_ready, c + 1)
            split_product(bank(p, SC)[:, 0:P], kT, qT, True, True,
                          [(lambda t, k=k: t[:, k, :], lambda t, k=k: t[:, k, :]) for k in range(KT)]).then_inc(s_done, 1)
            if nxt:
                project(i, p + 1, Q_, PQ, pq_done)
            pe.wait_ge(slo_ready, c + 1)
            pe.wait_ge(vNlo_ready, c + 1)
            mm = split_product(bank(p, OO)[:], sT, vN, True, first, [(lambda t: t[:], lambda t: t[:])])
            if not first:
                pe.wait_ge(kvlo_ready, KT * c)
                mm = split_product(bank(p, OO)[:], qT, kv, False, True,
                                   [(lambda t, k=k: t[:, k, :], lambda t, k=k: t[:, k, :]) for k in range(KT)])
            mm.then_inc(o_done, 1)
            if nxt:
                pe.wait_ge(kNlo_ready, c + 1)
                for t in range(KT):
                    split_product(state[t][:], kN, vN, first, True,
                                  [(lambda a, t=t: a[:, t * P:(t + 1) * P], lambda a: a[:])]).then_inc(state_done, 1)
            pe.wait_ge(og_ready, c + 1)
            if nxt:
                pe.wait_ge(k_ready, c + 2)
            transposes(bank(p, TOG), og32, tog_done)
            if nxt:
                project(i, p + 1, G_, PG, pg_done)
            pe.wait_ge(ogTlo_ready, c + 1)
            if nxt:
                pe.wait_ge(q_ready, c + 2)
            split_product(bank(p, WP)[:], ogT, w_out, True, True,
                          [(lambda t, k=k: t[:, k, :], lambda t, k=k: t[:, k, :]) for k in range(KT)]).then_inc(wp_done, 1)
            if nxt:
                project(i, p + 1, V_, PV, pv_done)

        pe.wait_ge(consts_ready, 3)
        pe.wait_ge(xT_loaded[0], 32)
        for n, (which, use, done) in enumerate(((K_, PK, pk_done), (Q_, PQ, pq_done), (G_, PG, pg_done), (V_, PV, pv_done))):
            pe.wait_ge(wlo_ready, n + 1)
            project(0, 0, which, use, done)
        pe.wait_ge(wlo_ready, 5)
        for p in range(UNROLL):
            step(0, p, first=p == 0)
        with pe.Fori(1, CHUNKS // UNROLL - 1) as i:
            for p in range(UNROLL):
                step(i, p)
        for p in range(UNROLL):
            step(CHUNKS // UNROLL - 1, p, last=True)

        def expand(b, slot, t):
            tile = b * ET + t
            pe.wait_ge(h_ready, tile + 1)
            for m, (dst, done) in enumerate(((work[t % 2], up_done), (work[2 + t % 2], gate_done))):
                for part in range(2):
                    for k in range(KT):
                        mm = pe.matmul(dst[:], codes[:, m * ET + t, k * P:(k + 1) * P], yT[slot][:, part, k, :],
                                       start=part == 0 and k == 0, stop=part == 1 and k == KT - 1)
                mm.then_inc(done, 1)

        def contract(b, t):
            if t == 0:
                pe.wait_ge(z_read, TT * (b + 1))
            pe.wait_ge(hlo_ready, b * ET + t + 1)
            for part in range(2):
                for tt in range(TT):
                    mm = pe.matmul(state[tt][:], hT[part][:, t % 2, tt * P:(tt + 1) * P], codes[:, 2 * ET + t, :],
                                   start=t == 0 and part == 0, stop=t == ET - 1 and part == 1, skip_group_check=True)
            mm.then_inc(down_done, 1)

        def ffn_block(b, b2, slot, last=False):
            for t in range(ET):
                if t < ET - 1:
                    expand(b, slot, t + 1)
                elif not last:
                    pe.wait_ge(yT_loaded[1 - slot], 32 * (b2 + slot + 1))
                    expand(b + 1, 1 - slot, 0)
                contract(b, t)

        pe.wait_ge(u_ready, CHUNKS)
        pe.wait_ge(piece_coded, UNROLL + PIECES)
        pe.wait_ge(yT_loaded[0], 32)
        expand(0, 0, 0)
        with pe.Fori(0, BLOCKS // 2 - 1) as i:
            for s in range(2):
                ffn_block(i * 2 + s, i, s)
        ffn_block(BLOCKS - 2, BLOCKS // 2 - 1, 0)
        ffn_block(BLOCKS - 1, BLOCKS // 2 - 1, 1, last=True)

    @block.scalar
    def _(act):
        def square_x(i, p):
            c, _, c4, slot = at(i, p)
            act.wait_ge(x_loaded[slot], 16 * (c4 + 1))
            act.wait_ge(ssq_ready, c)
            act.activation(squares[:], x32[:, slot, :], ACT.Square, accum_out=ssq[:, slot % 2:slot % 2 + 1]).then_inc(ssq_ready, 1)

        def norm_x(i, p):
            c, c2, _, slot = at(i, p)
            act.wait_ge(rms_ready, c + 1)
            if not (isinstance(c, int) and c == 0):
                pc, pc2, _, pslot = at(i, p - 1)
                act.wait_ge(xT_loaded[pslot % 2], 32 * (pc2 + 1))
            act.activation(xn[:, 0, :], x32[:, slot, :], ACT.Copy, scale=rms[:, slot % 2:slot % 2 + 1]).then_inc(xhi_ready, 1)

        def project_k(c, p):
            act.wait_ge(pk_done, c + 1)
            act.wait_ge(kNlo_ready, c)
            act.activation(k32[:], bank(p - 1, PK)[:], ACT.Silu, scale=wunscale[:, K_:K_ + 1]).then_inc(k_ready, 1)

        def project_q(c, p):
            act.wait_ge(pq_done, c + 1)
            act.activation(q32[:], bank(p - 1, PQ)[:], ACT.Silu, scale=wunscale[:, Q_:Q_ + 1]).then_inc(q_ready, 1)

        def project_g(c, p):
            act.wait_ge(pg_done, c + 1)
            act.wait_ge(og_ready, c)
            act.activation(gate_t[:], bank(p - 1, PG)[:], ACT.Tanh, scale=wunscale[:, G_:G_ + 1]).then_inc(g_ready, 1)

        def project_v(c, p):
            act.wait_ge(pv_done, c + 1)
            act.wait_ge(vNlo_ready, c)
            act.activation(v32[:], bank(p - 1, PV)[:], ACT.Silu, scale=wunscale[:, V_:V_ + 1]).then_inc(v_ready, 1)

        def sum_pieces(p, third):
            n = PER_STEP // 3
            for t in range(PER_STEP * p + n * third, PER_STEP * p + n * (third + 1)):
                act.wait_ge(piece_loaded[t % 4], 16 * (t // 4 + 1))
                act.wait_ge(abs_done, t)
                act.activation(junk[:], stage[:, t % 4, :], ACT.Abs, accum_out=asum[:, t:t + 1]).then_inc(abs_done, 1)

        def step(i, p, summing=False, last=False):
            c, _, _, _ = at(i, p)
            nxt = not (last and p == UNROLL - 1)
            act.wait_ge(tq_done, c + 1)
            act.activation(qT[0][:], bank(p, TQ)[:].rearrange("p (k t) -> p k t", k=KT), ACT.Copy).then_inc(qThi_ready, 1)
            act.wait_ge(tk_done, c + 1)
            act.activation(kT[0][:], bank(p, TK)[:].rearrange("p (k t) -> p k t", k=KT), ACT.Copy).then_inc(kThi_ready, 1)
            if not (last and p >= 2):
                square_x(i, p + 2)
            if summing:
                sum_pieces(p, 0)
            if nxt:
                project_k(c + 1, p + 1)
                project_q(c + 1, p + 1)
            if not (last and p >= 2):
                norm_x(i, p + 2)
            if summing:
                sum_pieces(p, 1)
            act.wait_ge(tog_done, c + 1)
            act.activation(ogT[0][:], bank(p, TOG)[:].rearrange("p (k t) -> p k t", k=KT), ACT.Copy).then_inc(ogThi_ready, 1)
            if nxt:
                for t in range(KT):
                    act.wait_ge(state_done, KT * c + t + 1)
                    act.activation(kv[0][:, t, :], state[t][:], ACT.Copy).then_inc(kvhi_ready, 1)
                project_g(c + 1, p + 1)
                if summing:
                    sum_pieces(p, 2)
                project_v(c + 1, p + 1)

        def split_weight(n):
            act.wait_ge(w_loaded[n % 2], 16 * (n // 2 + 1))
            src = stage[:, 2 * (n % 2):2 * (n % 2) + 2, :].rearrange("p a b -> p (a b)")
            if n < 4:
                act.wait_ge(small, 5 * (n + 1))
                act.activation(w_proj[:, n, 0].rearrange("p k d -> p (k d)"), src, ACT.Copy,
                               scale=wscale[:, n:n + 1]).then_inc(whi_ready, 1)
            else:
                act.activation(w_out[0][:].rearrange("p k d -> p (k d)"), src, ACT.Copy).then_inc(whi_ready, 1)

        square_x(0, 0)
        norm_x(0, 0)
        square_x(0, 1)
        split_weight(K_)
        split_weight(Q_)
        project_k(0, 0)
        norm_x(0, 1)
        project_q(0, 0)
        split_weight(G_)
        project_g(0, 0)
        split_weight(V_)
        project_v(0, 0)
        split_weight(4)
        for p in range(UNROLL):
            step(0, p, summing=True)
        with act.Fori(1, CHUNKS // UNROLL - 1) as i:
            for p in range(UNROLL):
                step(i, p)
        for p in range(UNROLL):
            step(CHUNKS // UNROLL - 1, p, last=True)

        act.wait_ge(small, 30)

        def tile(b, t):
            n = b * ET + t
            act.wait_ge(up_done, n + 1)
            act.wait_ge(h_ready, n + 1)
            act.activation(silu_u[:, t % 2, :], work[t % 2][:], ACT.Silu, scale=ffn_scale[:, 0:1]).then_inc(silu_ready, 1)
            act.wait_ge(h_ready, n + 3)
            if not (isinstance(n, int) and n < 2):
                act.wait_ge(down_done, n - 1)
            act.activation(hT[0][:, t % 2, :], h32[:], ACT.Copy).then_inc(hhi_ready, 1)

        for t in range(ET):
            tile(0, t)
        with act.Fori(1, BLOCKS) as b:
            for t in range(ET):
                tile(b, t)

    @block.vector
    def _(dve):
        def small_done(n):
            dve.wait_ge(small, n)

        def scale_of_weight(n):
            src = stage[:, 2 * (n % 2):2 * (n % 2) + 2, :].rearrange("p a b -> p (a b)")
            col = slice(n, n + 1)
            dve.wait_ge(w_loaded[n % 2], 16 * (n // 2 + 1))
            dve.tensor_reduce(wmax[:, col], src, AX.X, ALU.max, apply_absolute_value=True).then_inc(wmax_ready, 1)
            dve.wait_ge(wmax_all_ready, n + 1)
            dve.tensor_scalar(wmax_all[:, col], wmax_all[:, col], 2.0 ** -100, None, ALU.max).then_inc(small, 1)
            small_done(5 * n + 1)
            dve.tensor_scalar(wpow[:, col].bitcast(I32), wmax_all[:, col].bitcast(I32), EXPONENT_BITS, None,
                              ALU.bitwise_and).then_inc(small, 1)
            small_done(5 * n + 2)
            dve.reciprocal(winv[:, col], wpow[:, col]).then_inc(small, 1)
            small_done(5 * n + 3)
            dve.tensor_scalar(wscale[:, col], winv[:, col], W_SCALE, None, ALU.mult).then_inc(small, 1)
            dve.tensor_scalar(wunscale[:, col], wpow[:, col], (0.5 if n == G_ else 1.0) / (W_SCALE * ROW_SCALE), None,
                              ALU.mult).then_inc(small, 1)

        def split_weight(n):
            src = stage[:, 2 * (n % 2):2 * (n % 2) + 2, :].rearrange("p a b -> p (a b)")
            if n == 4:
                dve.wait_ge(w_loaded[0], 16 * 3)
            dve.wait_ge(whi_ready, n + 1)
            if n < 4:
                dve.scalar_tensor_tensor(out=w_proj[:, n, 1].rearrange("p k d -> p (k d)"), in0=src, scalar=wscale[:, n:n + 1],
                                         in1=w_proj[:, n, 0].rearrange("p k d -> p (k d)"), op0=ALU.mult,
                                         op1=ALU.subtract).then_inc(wlo_ready, 1)
            else:
                dve.tensor_tensor(w_out[1][:].rearrange("p k d -> p (k d)"), src,
                                  w_out[0][:].bitcast(F32).rearrange("p k d -> p (k d)"), ALU.subtract).then_inc(wlo_ready, 1)

        def norm_x(i, p):
            c, _, _, slot = at(i, p)
            dve.wait_ge(xhi_ready, c + 1)
            dve.scalar_tensor_tensor(out=xn[:, 1, :], in0=x32[:, slot, :], scalar=rms[:, slot % 2:slot % 2 + 1],
                                     in1=xn[:, 0, :], op0=ALU.mult, op1=ALU.subtract).then_inc(xlo_ready, 1)

        def split_k(c):
            dve.wait_ge(k_ready, c + 1)
            dve.tensor_copy(kN[0][:], k32[:]).then_inc(kNhi_ready, 1)
            dve.wait_ge(kNhi_ready, c + 1)
            dve.tensor_tensor(kN[1][:], k32[:], kN[0][:].bitcast(F32), ALU.subtract).then_inc(kNlo_ready, 1)

        def split_v(c):
            dve.wait_ge(v_ready, c + 1)
            dve.tensor_copy(vN[0][:], v32[:]).then_inc(vNhi_ready, 1)
            dve.wait_ge(vNhi_ready, c + 1)
            dve.tensor_tensor(vN[1][:], v32[:], vN[0][:].bitcast(F32), ALU.subtract).then_inc(vNlo_ready, 1)

        def low_of(dst, src, hi, hi_ready, value, done):
            dve.wait_ge(hi_ready, value)
            dve.tensor_tensor(dst, src, hi.bitcast(F32), ALU.subtract).then_inc(done, 1)

        def store_norm(i, p):
            c, _, _, _ = at(i, p)
            dve.wait_ge(rstd_ready, c + 1)
            dve.wait_ge(y_stored, 48 * c)
            dve.tensor_scalar(y32[:], u32[:], ln[:, 0, 0:1], rstd[:, 0:1], ALU.subtract, ALU.mult).then_inc(y_ready, 1)
            dve.wait_ge(y_ready, c + 1)
            dve.tensor_scalar(yhl[:, 0, :], y32[:], ROW_SCALE, None, ALU.mult).then_inc(yhi_ready, 1)
            dve.wait_ge(yhi_ready, c + 1)
            dve.scalar_tensor_tensor(out=yhl[:, 1, :], in0=y32[:], scalar=ROW_SCALE, in1=yhl[:, 0, :],
                                     op0=ALU.mult, op1=ALU.subtract).then_inc(ylo_ready, 1)

        def step(i, p, first=False, coding=False, last=False):
            c, _, _, _ = at(i, p)
            nxt = not (last and p == UNROLL - 1)
            low_of(qT[1][:], bank(p, TQ)[:].rearrange("p (k t) -> p k t", k=KT), qT[0][:], qThi_ready, c + 1, qTlo_ready)
            low_of(kT[1][:], bank(p, TK)[:].rearrange("p (k t) -> p k t", k=KT), kT[0][:], kThi_ready, c + 1, kTlo_ready)
            dve.wait_ge(s_done, c + 1)
            dve.tensor_tensor(sT32[:], bank(p, SC)[:, 0:P], causal[:], ALU.mult).then_inc(s_masked, 1)
            dve.wait_ge(s_masked, c + 1)
            dve.tensor_copy(sT[0][:], sT32[:]).then_inc(shi_ready, 1)
            dve.wait_ge(shi_ready, c + 1)
            dve.tensor_tensor(sT[1][:], sT32[:], sT[0][:].bitcast(F32), ALU.subtract).then_inc(slo_ready, 1)
            if not first:
                store_norm(i, p - 1)
            if coding:
                dve.wait_ge(piece_loaded[p], 16 * (PER_STEP + i))
                if p == 0:
                    dve.wait_ge(thr_ready, 1)
                dve.wait_ge(piece_coded, c)
                piece = c - UNROLL
                dve.tensor_scalar(below[:], stage[:, p, :], nthr[:, bass.ts(piece, 1)], None, ALU.is_lt).then_inc(below_ready, 1)
                dve.wait_ge(below_ready, piece + 1)
                dve.scalar_tensor_tensor(out=codes[:, bass.ts(piece, 2), :].rearrange("p a b -> p (a b)"),
                                         in0=stage[:, p, :], scalar=thr[:, bass.ts(piece, 1)], in1=below[:],
                                         op0=ALU.is_gt, op1=ALU.subtract).then_inc(piece_coded, 1)
            if not (last and p >= 2):
                norm_x(i, p + 2)
            dve.wait_ge(o_done, c + 1)
            dve.scalar_tensor_tensor(out=og32[:], in0=gate_t[:], scalar=1.0, in1=bank(p, OO)[:],
                                     op0=ALU.add, op1=ALU.mult).then_inc(og_ready, 1)
            low_of(ogT[1][:], bank(p, TOG)[:].rearrange("p (k t) -> p k t", k=KT), ogT[0][:], ogThi_ready, c + 1, ogTlo_ready)
            if nxt:
                for t in range(KT):
                    low_of(kv[1][:, t, :], state[t][:], kv[0][:, t, :], kvhi_ready, KT * c + t + 1, kvlo_ready)
                split_k(c + 1)
            dve.wait_ge(wp_done, c + 1)
            dve.scalar_tensor_tensor(out=u32[:], in0=bank(p, WP)[:], scalar=0.5, in1=x32[:, p % UNROLL, :],
                                     op0=ALU.mult, op1=ALU.add).then_inc(u_ready, 1)
            dve.wait_ge(u_ready, c + 1)
            dve.bn_stats(stats[:], u32[:]).then_inc(stats_ready, 1)
            dve.wait_ge(stats_ready, c + 1)
            carry(dve)
            dve.bn_aggr(ln[:, 0, :], stats[:]).then_inc(mv_ready, 1)
            if nxt:
                split_v(c + 1)

        def thresholds():
            dve.wait_ge(abs_done, PIECES)
            dve.tensor_reduce(msum[:, 0:MATS], asum[:].rearrange("p (m j) -> p m j", m=MATS), AX.X, ALU.add).then_inc(msum_ready, 1)
            dve.wait_ge(msum_all_ready, 1)
            dve.tensor_scalar(ffn_scale[:, 0:MATS], msum_all[:, 0:MATS], 1.0 / (D * E), QUANT_EPS, ALU.mult, ALU.add).then_inc(small, 1)
            small_done(21)
            for m in range(MATS):
                dve.tensor_scalar(nthr[:, m * PER_MAT:(m + 1) * PER_MAT], minus_half[:], ffn_scale[:, m:m + 1], None,
                                  ALU.mult).then_inc(small, 1)
            small_done(24)
            dve.tensor_scalar(thr[:], nthr[:], -1.0, None, ALU.mult).then_inc(thr_ready, 1)
            dve.reciprocal(ffn_scale[:, 5:6], ffn_scale[:, 0:1]).then_inc(small, 1)
            dve.tensor_tensor(ffn_scale[:, 6:7], ffn_scale[:, 0:1], ffn_scale[:, 1:2], ALU.mult).then_inc(small, 1)
            small_done(26)
            dve.tensor_scalar(ffn_scale[:, 3:4], ffn_scale[:, 5:6], 1.0 / (H_SCALE * ROW_SCALE), None, ALU.mult).then_inc(small, 1)
            dve.tensor_tensor(ffn_scale[:, 7:8], ffn_scale[:, 6:7], ffn_scale[:, 2:3], ALU.mult).then_inc(small, 1)
            small_done(28)
            dve.tensor_scalar(ffn_scale[:, 4:5], ffn_scale[:, 7:8], H_SCALE, None, ALU.mult).then_inc(small, 1)
            dve.tensor_scalar(ffn_scale[:, 0:1], ffn_scale[:, 0:1], 1.0 / ROW_SCALE, None, ALU.mult).then_inc(small, 1)

        dve.sem_inc(z_read, TT)
        dve.sem_inc(h_ready, 2)
        dve.sem_inc(piece_coded, UNROLL)
        dve.memset(minus_half[:], -0.5).then_inc(consts_ready, 1)
        scale_of_weight(K_)
        norm_x(0, 0)
        split_weight(K_)
        scale_of_weight(Q_)
        split_weight(Q_)
        norm_x(0, 1)
        split_k(0)
        scale_of_weight(G_)
        split_weight(G_)
        scale_of_weight(V_)
        split_weight(V_)
        split_weight(4)
        split_v(0)
        dve.wait_ge(consts_ready, 3)
        for p in range(UNROLL):
            step(0, p, first=p == 0)
        thresholds()
        with dve.Fori(1, CHUNKS // UNROLL - 1) as i:
            for p in range(UNROLL):
                step(i, p, coding=True)
        for p in range(UNROLL):
            step(CHUNKS // UNROLL - 1, p, last=True)
        store_norm(CHUNKS // UNROLL - 1, UNROLL - 1)

        def tile(b, t):
            n = b * ET + t
            dve.wait_ge(silu_ready, n + 1)
            dve.wait_ge(gate_done, n + 1)
            dve.wait_ge(hlo_ready, n)
            dve.scalar_tensor_tensor(out=h32[:], in0=silu_u[:, t % 2, :], scalar=ffn_scale[:, 3:4], in1=work[2 + t % 2][:],
                                     op0=ALU.mult, op1=ALU.mult).then_inc(h_ready, 1)
            dve.wait_ge(hhi_ready, n + 1)
            dve.tensor_tensor(hT[1][:, t % 2, :], h32[:], hT[0][:, t % 2, :], ALU.subtract).then_inc(hlo_ready, 1)

        def residual(b, b2, slot):
            dve.wait_ge(res_loaded[slot], 16 * (b2 + 1))
            dve.wait_ge(down_done, ET * (b + 1))
            for tt in range(TT):
                dve.scalar_tensor_tensor(out=res[slot][:, tt, :], in0=state[tt][:], scalar=ffn_scale[:, 4:5],
                                         in1=res[slot][:, tt, :], op0=ALU.mult, op1=ALU.add).then_inc(z_read, 1)

        def norm_stats(b, slot):
            for tt in range(TT):
                dve.wait_ge(z_read, TT * (b + 1) + tt + 1)
                dve.bn_stats(stats2[:, tt, :], res[slot][:, tt, :]).then_inc(stats2_ready, 1)
            for tt in range(TT):
                dve.wait_ge(stats2_ready, TT * b + tt + 1)
                carry(dve)
                bn = dve.bn_aggr(ln2[:, tt, :], stats2[:, tt, :])
            bn.then_inc(mv2_ready, 1)

        def norm_out(b, slot):
            dve.wait_ge(rstd2_ready, b + 1)
            for tt in range(TT):
                ins = dve.tensor_scalar(res[slot][:, tt, :], res[slot][:, tt, :], ln2[:, tt, 0:1], rstd2[:, tt:tt + 1],
                                        ALU.subtract, ALU.mult)
            ins.then_inc(out_ready, 1)

        def ffn_block(b, b2, slot, first=False):
            for t in range(ET):
                tile(b, t)
                if not first:
                    if t == 0:
                        residual(b - 1, b2 - (1 - slot), 1 - slot)
                    if t == 1:
                        norm_stats(b - 1, 1 - slot)
                    if t == 3:
                        norm_out(b - 1, 1 - slot)

        ffn_block(0, 0, 0, first=True)
        ffn_block(1, 0, 1)
        with dve.Fori(1, BLOCKS // 2) as i:
            for s in range(2):
                ffn_block(i * 2 + s, i, s)
        residual(BLOCKS - 1, BLOCKS // 2 - 1, 1)
        norm_stats(BLOCKS - 1, 1)
        norm_out(BLOCKS - 1, 1)

    @block.gpsimd
    def _(pool):
        pool.memset(causal[:], 1.0).then_inc(fill_done, 1)
        pool.memset(ident[:], 0.0).then_inc(fill_done, 1)
        pool.wait_ge(fill_done, 2)
        pool.affine_select(out=causal[:], in_=causal[:], compare_op=ALU.is_ge, fill=0.0, base=0, pattern=[[1, P]],
                           channel_multiplier=-1).then_inc(consts_ready, 1)
        pool.affine_select(out=ident[:], in_=ident[:], compare_op=ALU.not_equal, fill=1.0, base=0, pattern=[[1, P]],
                           channel_multiplier=-1).then_inc(consts_ready, 1)
        pool.wait_ge(consts_ready, 3)

        def rms_of(i, p):
            c, _, _, slot = at(i, p)
            col = slice(slot % 2, slot % 2 + 1)
            pool.wait_ge(ssq_ready, c + 1)
            carry(pool)
            s2 = ROW_SCALE * ROW_SCALE
            pool.tensor_scalar(ssq[:, col], ssq[:, col], 1.0 / (D * s2), RMS_EPS / s2, ALU.mult, ALU.add).then_inc(ms_ready, 1)
            pool.wait_ge(ms_ready, c + 1)
            pool.tensor_tensor(rms[:, col], ssq[:, col], minus_half[:, 0:1], ALU.pow).then_inc(rms_ready, 1)

        def weight_max(n):
            pool.wait_ge(wmax_ready, n + 1)
            pool.partition_all_reduce(wmax_all[:, n:n + 1], wmax[:, n:n + 1], P, bass.bass_isa.ReduceOp.max).then_inc(wmax_all_ready, 1)

        def rstd_of(c):
            pool.wait_ge(mv_ready, c + 1)
            carry(pool)
            pool.tensor_scalar(ln[:, 0, 1:2], ln[:, 0, 1:2], LN_EPS, None, ALU.add).then_inc(vareps_ready, 1)
            pool.wait_ge(vareps_ready, c + 1)
            pool.tensor_tensor(rstd[:, 0:1], ln[:, 0, 1:2], minus_half[:, 0:1], ALU.pow).then_inc(rstd_ready, 1)

        def step(i, p, last=False):
            c, _, _, _ = at(i, p)
            if not (last and p >= 2):
                rms_of(i, p + 2)
            rstd_of(c)

        rms_of(0, 0)
        weight_max(K_)
        rms_of(0, 1)
        weight_max(Q_)
        weight_max(G_)
        weight_max(V_)
        for p in range(UNROLL):
            step(0, p)
        pool.wait_ge(msum_ready, 1)
        pool.partition_all_reduce(msum_all[:, 0:MATS], msum[:, 0:MATS], P, bass.bass_isa.ReduceOp.add).then_inc(msum_all_ready, 1)
        with pool.Fori(1, CHUNKS // UNROLL - 1) as i:
            for p in range(UNROLL):
                step(i, p)
        for p in range(UNROLL):
            step(CHUNKS // UNROLL - 1, p, last=True)
        with pool.Fori(0, BLOCKS) as b:
            pool.wait_ge(mv2_ready, b + 1)
            carry(pool)
            pool.tensor_scalar(ln2[:, :, 1:2], ln2[:, :, 1:2], LN_EPS, None, ALU.add).then_inc(vareps2_ready, 1)
            pool.wait_ge(vareps2_ready, b + 1)
            pool.tensor_tensor(rstd2[:], ln2[:, :, 1], minus_half[:, 0:TT], ALU.pow).then_inc(rstd2_ready, 1)

    ctx.close()


def kernel(**inputs):
    import concourse.bacc as bacc
    from concourse.bass_utils import run_bass_kernel_spmd

    f = {n: np.asarray(a) for n, a in inputs.items()}

    def contraction_first(w):
        o, i = w.shape
        return w.T.reshape(i // P, P, o).transpose(1, 0, 2)

    w_attn = np.stack([contraction_first(f[f"L0_attn_W{n}"]).reshape(P, 2, PIECE) for n in "kqgvp"])
    mats = [contraction_first(f[f"L0_ffn_W_{n}"]).reshape(P, KT, ET, P).transpose(0, 2, 1, 3).reshape(P, PER_MAT, PIECE)
            for n in ("up", "gate")] + [contraction_first(f["L0_ffn_W_down"]).reshape(P, PER_MAT, PIECE)]
    w_ffn = np.concatenate([m.transpose(1, 0, 2) for m in mats])
    arrays = {
        "x": np.ascontiguousarray(f["L0_attn_x"].reshape(CHUNKS, P, D)),
        "w_attn": np.ascontiguousarray(w_attn),
        "w_ffn": np.ascontiguousarray(w_ffn),
    }
    nc = bacc.Bacc("TRN2", target_bir_lowering=False, num_devices=1)
    args = [nc.dram_tensor(n, a.shape, mybir.dt.from_np(a.dtype), kind="ExternalInput").ap() for n, a in arrays.items()]
    out = nc.dram_tensor("out", (CHUNKS, P, D), F32, kind="ExternalOutput").ap()
    build(nc, *args, out)
    r = run_bass_kernel_spmd(nc, [arrays], core_ids=[0])
    return r.results[0]["out"].reshape(1, TOKENS, D)
```

```python
from contextlib import ExitStack

import numpy as np

import concourse.bass as bass
import concourse.mybir as mybir
from concourse.alu_op_type import AluOpType as ALU

ACT = mybir.ActivationFunctionType
AX = mybir.AxisListType
F32 = mybir.dt.float32
F32R = mybir.dt.float32r
F16 = mybir.dt.float16
I32 = mybir.dt.int32

P = 128
TOKENS, D, E = 4096, 512, 2048
KT = D // P
ET = E // P
CHUNKS = TOKENS // P
UNROLL = 4
BLOCK = 512
BLOCKS = TOKENS // BLOCK
TT = BLOCK // P

PIECE = 1024
MATS = 3
PIECES = MATS * D * E // (P * PIECE)
PER_MAT = PIECES // MATS
PER_STEP = PIECES // UNROLL

ROW_SCALE = 64.0
W_SCALE = 256.0
H_SCALE = 8.0
RMS_EPS = float(np.finfo(np.float32).eps)
LN_EPS = 1e-5
QUANT_EPS = 1e-8
EXPONENT_BITS = 0x7F800000
K_, Q_, G_, V_, OUT_ = range(5)


def at(i, p):
    i = i + p // UNROLL
    p = p % UNROLL
    return i * UNROLL + p, i * 2 + p // 2, i, p


def build(nc, x, w_attn, w_ffn, out):
    ctx = ExitStack()
    phase_a = ExitStack()

    def sem(name):
        return ctx.enter_context(nc.semaphore(name))

    def sb(name, shape, dt, where=ctx):
        return where.enter_context(nc.sbuf_tensor(name, shape, dt))

    y_dram = nc.dram_tensor("y_dram", (CHUNKS, P, D), F32, kind="Internal").ap()
    yh_dram = nc.dram_tensor("yh_dram", (CHUNKS, P, D), F16, kind="Internal").ap()
    yl_dram = nc.dram_tensor("yl_dram", (CHUNKS, P, D), F16, kind="Internal").ap()

    codes = sb("codes", [P, MATS * ET, D], F16)
    yT = [sb(f"yT{b}", [P, 2, KT, BLOCK], F16) for b in range(2)]
    ffn_scale = sb("ffn_scale", [P, 16], F32)
    asum = sb("asum", [P, PIECES], F32)
    thr = sb("thr", [P, PIECES], F32)
    nthr = sb("nthr", [P, PIECES], F32)
    minus_half = sb("minus_half", [P, PER_MAT], F32)
    ln = sb("ln", [P, 2, 2], F32)
    stats = sb("stats", [P, 6], F32)
    rstd = sb("rstd", [P, 2], F32)
    ln2 = sb("ln2", [P, TT, 2], F32)
    stats2 = sb("stats2", [P, TT, 6], F32)
    rstd2 = sb("rstd2", [P, TT], F32)

    w_proj = sb("w_proj", [P, 4, 2, KT, D], F16, phase_a)
    w_out = [sb(f"w_out_{n}", [P, KT, D], F32R, phase_a) for n in ("hi", "lo")]
    stage = sb("stage", [P, 4, PIECE], F32, phase_a)
    below = sb("below", [P, PIECE], F16, phase_a)
    kv = [sb(f"kv_{n}", [P, KT, D], F32R, phase_a) for n in ("hi", "lo")]
    x32 = sb("x32", [P, UNROLL, D], F32, phase_a)
    xn = sb("xn", [P, 2, D], F16, phase_a)
    xnT = sb("xnT", [P, 2, 2, KT, P], F16, phase_a)
    q32 = sb("q32", [P, D], F32, phase_a)
    k32 = sb("k32", [P, D], F32, phase_a)
    v32 = sb("v32", [P, D], F32, phase_a)
    qT_parts = sb("qT_parts", [P, KT, 2, P], F32R, phase_a)
    qT = [qT_parts[:, :, part, :] for part in range(2)]
    kT = [sb(f"kT_{n}", [P, KT, P], F32R, phase_a) for n in ("hi", "lo")]
    kN = [sb(f"kN_{n}", [P, D], F32R, phase_a) for n in ("hi", "lo")]
    vN = [sb(f"vN_{n}", [P, D], F32R, phase_a) for n in ("hi", "lo")]
    s_cross = sb("s_cross", [P, P], F32, phase_a)
    s_sum = sb("s_sum", [P, P], F32, phase_a)
    sT32 = sb("sT32", [P, P], F32, phase_a)
    sT = [sb(f"sT_{n}", [P, P], F32R, phase_a) for n in ("hi", "lo")]
    gate_t = sb("gate_t", [P, D], F32, phase_a)
    og32 = sb("og32", [P, D], F32, phase_a)
    ogT = [sb(f"ogT_{n}", [P, KT, P], F32R, phase_a) for n in ("hi", "lo")]
    u32 = sb("u32", [P, D], F32, phase_a)
    y32 = sb("y32", [P, D], F32, phase_a)
    yhl = sb("yhl", [P, 2, D], F16, phase_a)
    squares = sb("squares", [P, D], F16, phase_a)
    junk = sb("junk", [P, PIECE], F16, phase_a)
    causal = sb("causal", [P, P], F32, phase_a)
    ident = sb("ident", [P, P], F32, phase_a)
    wmax = sb("wmax", [P, 4], F32, phase_a)
    wmax_all = sb("wmax_all", [P, 4], F32, phase_a)
    wpow = sb("wpow", [P, 4], F32, phase_a)
    winv = sb("winv", [P, 4], F32, phase_a)
    wscale = sb("wscale", [P, 4], F32, phase_a)
    wunscale = sb("wunscale", [P, 4], F32, phase_a)
    msum = sb("msum", [P, 4], F32, phase_a)
    msum_all = sb("msum_all", [P, 4], F32, phase_a)
    ssq = sb("ssq", [P, 2], F32, phase_a)
    rms = sb("rms", [P, 2], F32, phase_a)
    phase_a.close()

    def raw_weight(n):
        return codes[:, 8 * n:8 * n + 8, :].bitcast(F32).rearrange("p a b -> p (a b)")

    res = [sb(f"res{b}", [P, TT, D], F32) for b in range(2)]
    silu_u = sb("silu_u", [P, 2, BLOCK], F32)
    h32 = sb("h32", [P, BLOCK], F32)
    hT = [sb(f"hT_{n}", [P, 2, BLOCK], F16) for n in ("hi", "lo")]

    state = [ctx.enter_context(nc.psum_tensor(f"state{t}", [P, D], F32)) for t in range(4)]
    work = [ctx.enter_context(nc.psum_tensor(f"work{t}", [P, D], F32)) for t in range(4)]

    USES = 10
    TQ, TK, PK, SC, PQ, OO, TOG, PG, WP, PV = range(USES)

    def bank(p, use):
        return work[(USES * p + use) % 4]

    def bank_of(p, end):
        return (lambda use: state[{TQ: 0, TK: 1, SC: 2, OO: 3, TOG: 0, WP: 1}[use]]) if end else (lambda use: bank(p, use))

    consts_ready = sem("consts_ready")
    passed = sem("passed")
    fill_done = sem("fill_done")
    w_loaded = [sem(f"w_loaded{n}") for n in range(5)]
    wmax_ready, wmax_all_ready = sem("wmax_ready"), sem("wmax_all_ready")
    small = sem("small")
    whi_ready, wlo_ready, w_out_ready = sem("whi_ready"), sem("wlo_ready"), sem("w_out_ready")
    piece_loaded = [sem(f"piece_loaded{s}") for s in range(4)]
    abs_done, msum_ready, msum_all_ready, thr_ready = (sem(n) for n in ("abs_done", "msum_ready", "msum_all_ready", "thr_ready"))
    below_ready, piece_coded = sem("below_ready"), sem("piece_coded")
    x_loaded = [sem(f"x_loaded{s}") for s in range(UNROLL)]
    ssq_ready, ms_ready, rms_ready = sem("ssq_ready"), sem("ms_ready"), sem("rms_ready")
    xhi_ready, xlo_ready = sem("xhi_ready"), sem("xlo_ready")
    xT_loaded = [sem(f"xT_loaded{s}") for s in range(2)]
    pk_done, pq_done, pg_done, pv_done = (sem(n) for n in ("pk_done", "pq_done", "pg_done", "pv_done"))
    k_ready, q_ready, g_ready, v_ready = (sem(n) for n in ("k_ready", "q_ready", "g_ready", "v_ready"))
    tq_done, tk_done, tog_done = (sem(n) for n in ("tq_done", "tk_done", "tog_done"))
    qThi_ready, qTlo_ready = sem("qThi_ready"), sem("qTlo_ready")
    kThi_ready, kTlo_ready = sem("kThi_ready"), sem("kTlo_ready")
    ogThi_ready, ogTlo_ready = sem("ogThi_ready"), sem("ogTlo_ready")
    kNhi_ready, kNlo_ready = sem("kNhi_ready"), sem("kNlo_ready")
    vNhi_ready, vNlo_ready = sem("vNhi_ready"), sem("vNlo_ready")
    s_done, s_crossed, s_summed, s_masked, shi_ready, slo_ready = (
        sem(n) for n in ("s_done", "s_crossed", "s_summed", "s_masked", "shi_ready", "slo_ready"))
    o_done, og_ready = sem("o_done"), sem("og_ready")
    state_done, kvhi_ready, kvlo_ready = sem("state_done"), sem("kvhi_ready"), sem("kvlo_ready")
    wp_done, u_ready = sem("wp_done"), sem("u_ready")
    stats_ready, mv_ready, vareps_ready, rstd_ready = (sem(n) for n in ("stats_ready", "mv_ready", "vareps_ready", "rstd_ready"))
    y_ready, yhi_ready, ylo_ready = sem("y_ready"), sem("yhi_ready"), sem("ylo_ready")
    y_stored = sem("y_stored")
    yT_loaded = [sem(f"yT_loaded{b}") for b in range(2)]
    res_loaded = [sem(f"res_loaded{b}") for b in range(2)]
    up_done, gate_done, down_done = sem("up_done"), sem("gate_done"), sem("down_done")
    silu_ready, h_ready, hhi_ready, hlo_ready = (sem(n) for n in ("silu_ready", "h_ready", "hhi_ready", "hlo_ready"))
    z_read, stats2_ready, mv2_ready, vareps2_ready, rstd2_ready = (
        sem(n) for n in ("z_read", "stats2_ready", "mv2_ready", "vareps2_ready", "rstd2_ready"))
    out_ready = sem("out_ready")
    out_stored = [sem(f"out_stored{b}") for b in range(2)]

    block = ctx.enter_context(nc.Block())

    def carry(engine):
        engine.sem_inc(passed, 1)

    @block.sync
    def _(sp):
        def load_weight(n):
            sp.dma_start(raw_weight(n), w_attn[n]).then_inc(w_loaded[n], 16)

        def load_x(i, p):
            c, _, _, slot = at(i, p)
            sp.dma_start(x32[:, slot, :], x[c]).then_inc(x_loaded[slot], 16)

        def load_piece(t, slot):
            sp.dma_start(stage[:, slot, :], w_ffn[t]).then_inc(piece_loaded[slot], 16)

        def transpose_x(i, p):
            c, _, _, slot = at(i, p)
            sp.wait_ge(xhi_ready, c + 1)
            carry(sp)
            sp.dma_start(xnT[:, slot % 2, 0], xn[:, 0, :], transpose=True).then_inc(xT_loaded[slot % 2], 16)
            sp.wait_ge(xlo_ready, c + 1)
            carry(sp)
            sp.dma_start(xnT[:, slot % 2, 1], xn[:, 1, :], transpose=True).then_inc(xT_loaded[slot % 2], 16)

        def store_y(i, p):
            c, _, _, _ = at(i, p)
            sp.wait_ge(y_ready, c + 1)
            carry(sp)
            sp.dma_start(y_dram[c], y32[:]).then_inc(y_stored, 16)
            sp.wait_ge(yhi_ready, c + 1)
            carry(sp)
            sp.dma_start(yh_dram[c], yhl[:, 0, :]).then_inc(y_stored, 16)
            sp.wait_ge(ylo_ready, c + 1)
            carry(sp)
            sp.dma_start(yl_dram[c], yhl[:, 1, :]).then_inc(y_stored, 16)

        def load_transposed(b, slot):
            for part, src in enumerate((yh_dram, yl_dram)):
                sp.dma_start(yT[slot][:, part], src[bass.ts(b, TT)].rearrange("t p d -> (t p) d"),
                             transpose=True).then_inc(yT_loaded[slot], 16)

        def load_rows(b, slot):
            sp.dma_start(res[slot][:], y_dram[bass.ts(b, TT)].rearrange("t p d -> p t d")).then_inc(res_loaded[slot], 16)

        def store_block(b, slot):
            sp.wait_ge(out_ready, TT * (b + 1))
            carry(sp)
            sp.dma_start(out[bass.ts(b, TT)].rearrange("t p d -> p t d"), res[slot][:]).then_inc(out_stored[slot], 16)

        def step(i, p, first=False, summing=False, coding=False, last=False):
            c, _, _, _ = at(i, p)
            if summing:
                for t in range(PER_STEP * p, PER_STEP * (p + 1)):
                    if t >= 4:
                        sp.wait_ge(abs_done, t - 3)
                    load_piece(t, t % 4)
            if coding:
                if p == 0:
                    sp.wait_ge(abs_done, PIECES)
                sp.wait_ge(piece_coded, c - UNROLL + 1)
                carry(sp)
                load_piece(c - UNROLL, p)
            if last and p == 1:
                sp.wait_ge(y_stored, 48 * (CHUNKS - UNROLL))
                load_transposed(0, 0)
                load_transposed(1, 1)
            if not first:
                store_y(i, p - 1)
            if not (last and p >= 2):
                sp.wait_ge(pv_done, c + 1)
                carry(sp)
                transpose_x(i, p + 2)
            if not last:
                sp.wait_ge(u_ready, c + 1)
                carry(sp)
                load_x(i, p + UNROLL)

        load_x(0, 0)
        load_weight(K_)
        load_weight(Q_)
        load_x(0, 1)
        transpose_x(0, 0)
        load_weight(G_)
        load_weight(V_)
        load_weight(OUT_)
        load_x(0, 2)
        load_x(0, 3)
        transpose_x(0, 1)
        for p in range(UNROLL):
            step(0, p, first=p == 0, summing=True)
        with sp.Fori(1, CHUNKS // UNROLL - 1) as i:
            for p in range(UNROLL):
                step(i, p, coding=True)
        for p in range(UNROLL):
            step(CHUNKS // UNROLL - 1, p, last=True)
        store_y(CHUNKS // UNROLL - 1, UNROLL - 1)

        sp.wait_ge(y_stored, 48 * CHUNKS)
        load_rows(0, 0)
        load_rows(1, 1)
        with sp.Fori(0, BLOCKS // 2 - 1) as i:
            for s in range(2):
                b = i * 2 + s
                store_block(b, s)
                load_transposed(b + 2, s)
                sp.wait_ge(out_stored[s], 16 * (i + 1))
                carry(sp)
                load_rows(b + 2, s)
        store_block(BLOCKS - 2, 0)
        for tt in range(TT):
            sp.wait_ge(out_ready, TT * (BLOCKS - 1) + tt + 1)
            sp.dma_start(out[TT * (BLOCKS - 1) + tt], res[1][:, tt, :]).then_inc(out_stored[1], 16)
        sp.wait_ge(out_stored[0], 16 * (BLOCKS // 2))
        sp.wait_ge(out_stored[1], 16 * (BLOCKS // 2 - 1 + TT))

    @block.tensor
    def _(pe):
        PARTS = ((0, 0), (0, 1), (1, 0))

        def project(i, p, which, use, done):
            _, _, _, slot = at(i, p)
            dst = bank(p - 1, use)
            for k in range(KT):
                for n, (a, b) in enumerate(PARTS):
                    mm = pe.matmul(dst[:], xnT[:, slot % 2, a, k, :], w_proj[:, which, b, k, :],
                                   start=n == 0 and k == 0, stop=n == 2 and k == KT - 1)
            mm.then_inc(done, 1)

        def transposes(dst, src, done):
            for k in range(KT):
                mm = pe.transpose(dst[:, k * P:(k + 1) * P], src[:, k * P:(k + 1) * P], ident[:])
            mm.then_inc(done, 1)

        def split_product(dst, lhs, rhs, start, stop):
            for n, (a, b) in enumerate(PARTS):
                mm = pe.matmul(dst, lhs[a], rhs[b], start=start and n == 0, stop=stop and n == 2, skip_group_check=True)
            return mm

        def tiles(t, n):
            return [t[0][:, n, :], t[1][:, n, :]]

        def step(i, p, first=False, last=False):
            c, _, _, _ = at(i, p)
            end = last and p == UNROLL - 1
            my = bank_of(p, end)
            if end:
                pe.wait_ge(kvlo_ready, KT * c)
            elif first:
                pe.wait_ge(k_ready, 1)
            else:
                pe.wait_ge(ogTlo_ready, c)
            pe.wait_ge(q_ready, c + 1)
            transposes(my(TQ), q32, tq_done)
            pe.wait_ge(k_ready, c + 1)
            if not end:
                pe.wait_ge(g_ready, c + 1)
            transposes(my(TK), k32, tk_done)
            if not first:
                pe.wait_ge(u_ready, c)
            if end:
                pe.wait_ge(yT_loaded[0], 32)
                expand(0, 0, 0, UP)
            else:
                _, c2, _, slot = at(i, p + 1)
                pe.wait_ge(xT_loaded[slot % 2], 32 * (c2 + 1))
                project(i, p + 1, K_, PK, pk_done)
            pe.wait_ge(qTlo_ready, c + 1)
            pe.wait_ge(kTlo_ready, c + 1)
            if not end:
                pe.wait_ge(v_ready, c + 1)
            for k in range(KT):
                pe.matmul(my(SC)[:, 0:2 * P], kT[0][:, k, :], qT_parts[:, k].rearrange("p a t -> p (a t)"),
                          start=k == 0, stop=k == KT - 1, skip_group_check=True)
                mm = pe.matmul(my(SC)[:, 0:P], kT[1][:, k, :], qT[0][:, k, :], start=False, stop=k == KT - 1,
                               skip_group_check=True)
            mm.then_inc(s_done, 1)
            if end:
                pe.wait_ge(ogTlo_ready, c)
                pe.wait_ge(piece_coded, UNROLL + PIECES)
                expand(0, 0, 0, GATE)
            else:
                project(i, p + 1, Q_, PQ, pq_done)
            pe.wait_ge(slo_ready, c + 1)
            pe.wait_ge(vNlo_ready, c + 1)
            mm = split_product(my(OO)[:], [sT[0][:], sT[1][:]], [vN[0][:], vN[1][:]], True, first)
            if not first:
                pe.wait_ge(kvlo_ready, KT * c)
                for k in range(KT):
                    mm = split_product(my(OO)[:], tiles(qT, k), tiles(kv, k), False, k == KT - 1)
            mm.then_inc(o_done, 1)
            if end:
                pe.wait_ge(v_ready, c + 1)
                expand(0, 0, 1, UP)
            else:
                pe.wait_ge(kNlo_ready, c + 1)
                for t in range(KT):
                    split_product(state[t][:], [part[:, t * P:(t + 1) * P] for part in kN], [vN[0][:], vN[1][:]],
                                  first, True).then_inc(state_done, 1)
                pe.wait_ge(k_ready, c + 2)
            pe.wait_ge(og_ready, c + 1)
            transposes(my(TOG), og32, tog_done)
            if end:
                pe.wait_ge(g_ready, c + 1)
                expand(0, 0, 1, GATE)
            else:
                project(i, p + 1, G_, PG, pg_done)
                pe.wait_ge(q_ready, c + 2)
            pe.wait_ge(ogTlo_ready, c + 1)
            if first:
                pe.wait_ge(w_out_ready, 1)
            for k in range(KT):
                mm = split_product(my(WP)[:], tiles(ogT, k), tiles(w_out, k), k == 0, k == KT - 1)
            mm.then_inc(wp_done, 1)
            if not end:
                project(i, p + 1, V_, PV, pv_done)

        UP, GATE = 0, 1

        def expand(b, slot, t, which):
            dst, done = (work[t % 2], up_done) if which == UP else (work[2 + t % 2], gate_done)
            for k in range(KT):
                for part in range(2):
                    mm = pe.matmul(dst[:], codes[:, which * ET + t, k * P:(k + 1) * P], yT[slot][:, part, k, :],
                                   start=part == 0 and k == 0, stop=part == 1 and k == KT - 1)
            mm.then_inc(done, 1)

        pe.wait_ge(consts_ready, 3)
        pe.wait_ge(xT_loaded[0], 32)
        for n, (which, use, done) in enumerate(((K_, PK, pk_done), (Q_, PQ, pq_done), (G_, PG, pg_done), (V_, PV, pv_done))):
            pe.wait_ge(wlo_ready, n + 1)
            project(0, 0, which, use, done)
        for p in range(UNROLL):
            step(0, p, first=p == 0)
        with pe.Fori(1, CHUNKS // UNROLL - 1) as i:
            for p in range(UNROLL):
                step(i, p)
        for p in range(UNROLL):
            step(CHUNKS // UNROLL - 1, p, last=True)

        def contract(b, t):
            pe.wait_ge(hlo_ready, b * ET + t + 1)
            for tt in range(TT):
                if t == 0:
                    pe.wait_ge(z_read, TT * b + tt + 1)
                for part in range(2):
                    mm = pe.matmul(state[tt][:], hT[part][:, t % 2, tt * P:(tt + 1) * P], codes[:, 2 * ET + t, :],
                                   start=t == 0 and part == 0, stop=t == ET - 1 and part == 1, skip_group_check=True)
                mm.then_inc(down_done, 1)

        def ffn_block(b, b2, slot, last=False):
            for t in range(ET):
                ahead = (t + 2) % ET
                if not (last and ahead < 2):
                    nb, nslot = (b, slot) if t < ET - 2 else (b + 1, 1 - slot)
                    if t == ET - 2:
                        pe.wait_ge(yT_loaded[1 - slot], 32 * (b2 + slot + 1))
                    pe.wait_ge(h_ready, nb * ET + ahead + 1)
                    expand(nb, nslot, ahead, UP)
                    expand(nb, nslot, ahead, GATE)
                contract(b, t)

        pe.wait_ge(u_ready, CHUNKS)
        with pe.Fori(0, BLOCKS // 2 - 1) as i:
            for s in range(2):
                ffn_block(i * 2 + s, i, s)
        ffn_block(BLOCKS - 2, BLOCKS // 2 - 1, 0)
        ffn_block(BLOCKS - 1, BLOCKS // 2 - 1, 1, last=True)

    @block.scalar
    def _(act):
        def square_x(i, p):
            c, _, c4, slot = at(i, p)
            act.wait_ge(x_loaded[slot], 16 * (c4 + 1))
            act.wait_ge(ssq_ready, c)
            act.activation(squares[:], x32[:, slot, :], ACT.Square, accum_out=ssq[:, slot % 2:slot % 2 + 1]).then_inc(ssq_ready, 1)

        def norm_x(i, p):
            c, c2, _, slot = at(i, p)
            act.wait_ge(rms_ready, c + 1)
            if not (isinstance(c, int) and c == 0):
                pc, pc2, _, pslot = at(i, p - 1)
                act.wait_ge(xT_loaded[pslot % 2], 32 * (pc2 + 1))
            act.activation(xn[:, 0, :], x32[:, slot, :], ACT.Copy, scale=rms[:, slot % 2:slot % 2 + 1]).then_inc(xhi_ready, 1)

        def project_k(c, p):
            act.wait_ge(pk_done, c + 1)
            act.wait_ge(kNlo_ready, c)
            act.activation(k32[:], bank(p - 1, PK)[:], ACT.Silu, scale=wunscale[:, K_:K_ + 1]).then_inc(k_ready, 1)

        def project_q(c, p):
            act.wait_ge(pq_done, c + 1)
            act.activation(q32[:], bank(p - 1, PQ)[:], ACT.Silu, scale=wunscale[:, Q_:Q_ + 1]).then_inc(q_ready, 1)

        def project_g(c, p):
            act.wait_ge(pg_done, c + 1)
            act.wait_ge(og_ready, c)
            act.activation(gate_t[:], bank(p - 1, PG)[:], ACT.Tanh, scale=wunscale[:, G_:G_ + 1]).then_inc(g_ready, 1)

        def project_v(c, p):
            act.wait_ge(pv_done, c + 1)
            act.wait_ge(vNlo_ready, c)
            act.activation(v32[:], bank(p - 1, PV)[:], ACT.Silu, scale=wunscale[:, V_:V_ + 1]).then_inc(v_ready, 1)

        def sum_pieces(p, third):
            n = PER_STEP // 3
            for t in range(PER_STEP * p + n * third, PER_STEP * p + n * (third + 1)):
                act.wait_ge(piece_loaded[t % 4], 16 * (t // 4 + 1))
                act.wait_ge(abs_done, t)
                act.activation(junk[:], stage[:, t % 4, :], ACT.Abs, accum_out=asum[:, t:t + 1]).then_inc(abs_done, 1)

        def step(i, p, summing=False, last=False):
            c, _, _, _ = at(i, p)
            nxt = not (last and p == UNROLL - 1)
            my = bank_of(p, not nxt)
            act.wait_ge(tq_done, c + 1)
            act.activation(qT[0], my(TQ)[:].rearrange("p (k t) -> p k t", k=KT), ACT.Copy).then_inc(qThi_ready, 1)
            act.wait_ge(tk_done, c + 1)
            act.activation(kT[0][:], my(TK)[:].rearrange("p (k t) -> p k t", k=KT), ACT.Copy).then_inc(kThi_ready, 1)
            if not (last and p >= 2):
                square_x(i, p + 2)
            if summing:
                sum_pieces(p, 0)
            if nxt:
                project_k(c + 1, p + 1)
            if not (last and p >= 2):
                norm_x(i, p + 2)
            if nxt:
                project_q(c + 1, p + 1)
            if summing:
                sum_pieces(p, 1)
            act.wait_ge(tog_done, c + 1)
            act.activation(ogT[0][:], my(TOG)[:].rearrange("p (k t) -> p k t", k=KT), ACT.Copy).then_inc(ogThi_ready, 1)
            if nxt:
                for t in range(KT):
                    act.wait_ge(state_done, KT * c + t + 1)
                    act.activation(kv[0][:, t, :], state[t][:], ACT.Copy).then_inc(kvhi_ready, 1)
                project_g(c + 1, p + 1)
                if summing:
                    sum_pieces(p, 2)
                project_v(c + 1, p + 1)

        def split_weight(n):
            src = raw_weight(n)
            act.wait_ge(w_loaded[n], 16)
            if n < OUT_:
                act.wait_ge(small, 5 * (n + 1))
                act.activation(w_proj[:, n, 0].rearrange("p k d -> p (k d)"), src, ACT.Copy,
                               scale=wscale[:, n:n + 1]).then_inc(whi_ready, 1)
            else:
                act.activation(w_out[0][:].rearrange("p k d -> p (k d)"), src, ACT.Copy).then_inc(whi_ready, 1)

        square_x(0, 0)
        norm_x(0, 0)
        square_x(0, 1)
        split_weight(K_)
        split_weight(Q_)
        norm_x(0, 1)
        project_k(0, 0)
        split_weight(G_)
        project_q(0, 0)
        split_weight(V_)
        project_g(0, 0)
        split_weight(OUT_)
        project_v(0, 0)
        for p in range(UNROLL):
            step(0, p, summing=True)
        with act.Fori(1, CHUNKS // UNROLL - 1) as i:
            for p in range(UNROLL):
                step(i, p)
        for p in range(UNROLL):
            step(CHUNKS // UNROLL - 1, p, last=True)

        act.wait_ge(small, 30)

        def tile(b, t):
            n = b * ET + t
            act.wait_ge(up_done, n + 1)
            act.wait_ge(h_ready, n + 1)
            act.activation(silu_u[:, t % 2, :], work[t % 2][:], ACT.Silu, scale=ffn_scale[:, 0:1]).then_inc(silu_ready, 1)
            act.wait_ge(h_ready, n + 3)
            if not (isinstance(n, int) and n < 2):
                act.wait_ge(down_done, TT * (n - 1))
            act.activation(hT[0][:, t % 2, :], h32[:], ACT.Copy).then_inc(hhi_ready, 1)

        for t in range(ET):
            tile(0, t)
        with act.Fori(1, BLOCKS) as b:
            for t in range(ET):
                tile(b, t)

    @block.vector
    def _(dve):
        def small_done(n):
            dve.wait_ge(small, n)

        def largest_weight(n):
            dve.wait_ge(w_loaded[n], 16)
            dve.tensor_reduce(wmax[:, n:n + 1], raw_weight(n), AX.X, ALU.max, apply_absolute_value=True).then_inc(wmax_ready, 1)

        def scale_of_weight(n):
            col = slice(n, n + 1)
            dve.wait_ge(wmax_all_ready, n + 1)
            dve.tensor_scalar(wmax_all[:, col], wmax_all[:, col], 2.0 ** -100, None, ALU.max).then_inc(small, 1)
            small_done(5 * n + 1)
            dve.tensor_scalar(wpow[:, col].bitcast(I32), wmax_all[:, col].bitcast(I32), EXPONENT_BITS, None,
                              ALU.bitwise_and).then_inc(small, 1)
            small_done(5 * n + 2)
            dve.reciprocal(winv[:, col], wpow[:, col]).then_inc(small, 1)
            small_done(5 * n + 3)
            dve.tensor_scalar(wscale[:, col], winv[:, col], W_SCALE, None, ALU.mult).then_inc(small, 1)
            dve.tensor_scalar(wunscale[:, col], wpow[:, col], (0.5 if n == G_ else 1.0) / (W_SCALE * ROW_SCALE), None,
                              ALU.mult).then_inc(small, 1)

        def split_weight(n):
            dve.wait_ge(whi_ready, n + 1)
            dve.scalar_tensor_tensor(out=w_proj[:, n, 1].rearrange("p k d -> p (k d)"), in0=raw_weight(n),
                                     scalar=wscale[:, n:n + 1], in1=w_proj[:, n, 0].rearrange("p k d -> p (k d)"),
                                     op0=ALU.mult, op1=ALU.subtract).then_inc(wlo_ready, 1)

        def norm_x(i, p):
            c, _, _, slot = at(i, p)
            dve.wait_ge(xhi_ready, c + 1)
            dve.scalar_tensor_tensor(out=xn[:, 1, :], in0=x32[:, slot, :], scalar=rms[:, slot % 2:slot % 2 + 1],
                                     in1=xn[:, 0, :], op0=ALU.mult, op1=ALU.subtract).then_inc(xlo_ready, 1)

        def split_k(c):
            dve.wait_ge(k_ready, c + 1)
            dve.tensor_copy(kN[0][:], k32[:]).then_inc(kNhi_ready, 1)
            dve.wait_ge(kNhi_ready, c + 1)
            dve.tensor_tensor(kN[1][:], k32[:], kN[0][:].bitcast(F32), ALU.subtract).then_inc(kNlo_ready, 1)

        def split_v(c):
            dve.wait_ge(v_ready, c + 1)
            dve.tensor_copy(vN[0][:], v32[:]).then_inc(vNhi_ready, 1)
            dve.wait_ge(vNhi_ready, c + 1)
            dve.tensor_tensor(vN[1][:], v32[:], vN[0][:].bitcast(F32), ALU.subtract).then_inc(vNlo_ready, 1)

        def low_of(dst, src, hi, hi_ready, value, done):
            dve.wait_ge(hi_ready, value)
            dve.tensor_tensor(dst, src, hi.bitcast(F32), ALU.subtract).then_inc(done, 1)

        def store_norm(i, p):
            c, _, _, _ = at(i, p)
            dve.wait_ge(rstd_ready, c + 1)
            dve.wait_ge(y_stored, 48 * c)
            dve.tensor_scalar(y32[:], u32[:], ln[:, 0, 0:1], rstd[:, 0:1], ALU.subtract, ALU.mult).then_inc(y_ready, 1)
            dve.wait_ge(y_ready, c + 1)
            dve.tensor_scalar(yhl[:, 0, :], y32[:], ROW_SCALE, None, ALU.mult).then_inc(yhi_ready, 1)
            dve.wait_ge(yhi_ready, c + 1)
            dve.scalar_tensor_tensor(out=yhl[:, 1, :], in0=y32[:], scalar=ROW_SCALE, in1=yhl[:, 0, :],
                                     op0=ALU.mult, op1=ALU.subtract).then_inc(ylo_ready, 1)

        def tile(b, t):
            n = b * ET + t
            dve.wait_ge(silu_ready, n + 1)
            dve.wait_ge(gate_done, n + 1)
            dve.wait_ge(hlo_ready, n)
            dve.scalar_tensor_tensor(out=h32[:], in0=silu_u[:, t % 2, :], scalar=ffn_scale[:, 3:4], in1=work[2 + t % 2][:],
                                     op0=ALU.mult, op1=ALU.mult).then_inc(h_ready, 1)
            dve.wait_ge(hhi_ready, n + 1)
            dve.tensor_tensor(hT[1][:, t % 2, :], h32[:], hT[0][:, t % 2, :], ALU.subtract).then_inc(hlo_ready, 1)

        def step(i, p, first=False, coding=False, last=False):
            c, _, _, _ = at(i, p)
            nxt = not (last and p == UNROLL - 1)
            my = bank_of(p, not nxt)
            low_of(qT[1], my(TQ)[:].rearrange("p (k t) -> p k t", k=KT), qT[0], qThi_ready, c + 1, qTlo_ready)
            low_of(kT[1][:], my(TK)[:].rearrange("p (k t) -> p k t", k=KT), kT[0][:], kThi_ready, c + 1, kTlo_ready)
            dve.wait_ge(s_done, c + 1)
            dve.tensor_copy(s_cross[:], my(SC)[:, P:2 * P]).then_inc(s_crossed, 1)
            dve.wait_ge(s_crossed, c + 1)
            dve.tensor_tensor(s_sum[:], my(SC)[:, 0:P], s_cross[:], ALU.add).then_inc(s_summed, 1)
            dve.wait_ge(s_summed, c + 1)
            dve.tensor_tensor(sT32[:], s_sum[:], causal[:], ALU.mult).then_inc(s_masked, 1)
            dve.wait_ge(s_masked, c + 1)
            dve.tensor_copy(sT[0][:], sT32[:]).then_inc(shi_ready, 1)
            dve.wait_ge(shi_ready, c + 1)
            dve.tensor_tensor(sT[1][:], sT32[:], sT[0][:].bitcast(F32), ALU.subtract).then_inc(slo_ready, 1)
            if not first:
                store_norm(i, p - 1)
            if coding:
                dve.wait_ge(piece_loaded[p], 16 * (PER_STEP + i))
                if p == 0:
                    dve.wait_ge(thr_ready, 1)
                dve.wait_ge(piece_coded, c)
                piece = c - UNROLL
                dve.tensor_scalar(below[:], stage[:, p, :], nthr[:, bass.ts(piece, 1)], None, ALU.is_lt).then_inc(below_ready, 1)
                dve.wait_ge(below_ready, piece + 1)
                dve.scalar_tensor_tensor(out=codes[:, bass.ts(piece, 2), :].rearrange("p a b -> p (a b)"),
                                         in0=stage[:, p, :], scalar=thr[:, bass.ts(piece, 1)], in1=below[:],
                                         op0=ALU.is_gt, op1=ALU.subtract).then_inc(piece_coded, 1)
            if not (last and p >= 2):
                norm_x(i, p + 2)
            dve.wait_ge(o_done, c + 1)
            dve.scalar_tensor_tensor(out=og32[:], in0=gate_t[:], scalar=1.0, in1=my(OO)[:],
                                     op0=ALU.add, op1=ALU.mult).then_inc(og_ready, 1)
            low_of(ogT[1][:], my(TOG)[:].rearrange("p (k t) -> p k t", k=KT), ogT[0][:], ogThi_ready, c + 1, ogTlo_ready)
            if nxt:
                for t in range(KT):
                    low_of(kv[1][:, t, :], state[t][:], kv[0][:, t, :], kvhi_ready, KT * c + t + 1, kvlo_ready)
                split_k(c + 1)
            if not nxt:
                tile(0, 0)
            dve.wait_ge(wp_done, c + 1)
            dve.scalar_tensor_tensor(out=u32[:], in0=my(WP)[:], scalar=0.5, in1=x32[:, p % UNROLL, :],
                                     op0=ALU.mult, op1=ALU.add).then_inc(u_ready, 1)
            dve.wait_ge(u_ready, c + 1)
            dve.bn_stats(stats[:], u32[:]).then_inc(stats_ready, 1)
            dve.wait_ge(stats_ready, c + 1)
            carry(dve)
            dve.bn_aggr(ln[:, 0, :], stats[:]).then_inc(mv_ready, 1)
            if nxt:
                split_v(c + 1)

        def thresholds():
            dve.wait_ge(abs_done, PIECES)
            dve.tensor_reduce(msum[:, 0:MATS], asum[:].rearrange("p (m j) -> p m j", m=MATS), AX.X, ALU.add).then_inc(msum_ready, 1)
            dve.wait_ge(msum_all_ready, 1)
            dve.tensor_scalar(ffn_scale[:, 0:MATS], msum_all[:, 0:MATS], 1.0 / (D * E), QUANT_EPS, ALU.mult, ALU.add).then_inc(small, 1)
            small_done(21)
            for m in range(MATS):
                dve.tensor_scalar(nthr[:, m * PER_MAT:(m + 1) * PER_MAT], minus_half[:], ffn_scale[:, m:m + 1], None,
                                  ALU.mult).then_inc(small, 1)
            small_done(24)
            dve.tensor_scalar(thr[:], nthr[:], -1.0, None, ALU.mult).then_inc(thr_ready, 1)
            dve.reciprocal(ffn_scale[:, 5:6], ffn_scale[:, 0:1]).then_inc(small, 1)
            dve.tensor_tensor(ffn_scale[:, 6:7], ffn_scale[:, 0:1], ffn_scale[:, 1:2], ALU.mult).then_inc(small, 1)
            small_done(26)
            dve.tensor_scalar(ffn_scale[:, 3:4], ffn_scale[:, 5:6], 1.0 / (H_SCALE * ROW_SCALE), None, ALU.mult).then_inc(small, 1)
            dve.tensor_tensor(ffn_scale[:, 7:8], ffn_scale[:, 6:7], ffn_scale[:, 2:3], ALU.mult).then_inc(small, 1)
            small_done(28)
            dve.tensor_scalar(ffn_scale[:, 4:5], ffn_scale[:, 7:8], H_SCALE, None, ALU.mult).then_inc(small, 1)
            dve.tensor_scalar(ffn_scale[:, 0:1], ffn_scale[:, 0:1], 1.0 / ROW_SCALE, None, ALU.mult).then_inc(small, 1)

        dve.sem_inc(z_read, TT)
        dve.sem_inc(h_ready, 2)
        dve.sem_inc(piece_coded, UNROLL)
        dve.memset(minus_half[:], -0.5).then_inc(consts_ready, 1)
        largest_weight(K_)
        norm_x(0, 0)
        scale_of_weight(K_)
        largest_weight(Q_)
        split_weight(K_)
        scale_of_weight(Q_)
        largest_weight(G_)
        split_weight(Q_)
        norm_x(0, 1)
        scale_of_weight(G_)
        largest_weight(V_)
        split_weight(G_)
        scale_of_weight(V_)
        split_k(0)
        split_weight(V_)
        split_v(0)
        dve.wait_ge(consts_ready, 3)
        for p in range(UNROLL):
            step(0, p, first=p == 0)
        thresholds()
        with dve.Fori(1, CHUNKS // UNROLL - 1) as i:
            for p in range(UNROLL):
                step(i, p, coding=True)
        for p in range(UNROLL):
            step(CHUNKS // UNROLL - 1, p, last=True)

        def residual(b, b2, slot):
            dve.wait_ge(res_loaded[slot], 16 * (b2 + 1))
            for tt in range(TT):
                dve.wait_ge(down_done, TT * (ET * b + ET - 1) + tt + 1)
                dve.scalar_tensor_tensor(out=res[slot][:, tt, :], in0=state[tt][:], scalar=ffn_scale[:, 4:5],
                                         in1=res[slot][:, tt, :], op0=ALU.mult, op1=ALU.add).then_inc(z_read, 1)

        def norm_stats(b, slot, tts):
            for tt in tts:
                dve.wait_ge(z_read, TT * (b + 1) + tt + 1)
                dve.bn_stats(stats2[:, tt, :], res[slot][:, tt, :]).then_inc(stats2_ready, 1)

        def norm_moments(b):
            for tt in range(TT):
                dve.wait_ge(stats2_ready, TT * b + tt + 1)
                carry(dve)
                bn = dve.bn_aggr(ln2[:, tt, :], stats2[:, tt, :])
            bn.then_inc(mv2_ready, 1)

        def norm_out(b, slot, tts):
            dve.wait_ge(rstd2_ready, b + 1)
            for tt in tts:
                dve.tensor_scalar(res[slot][:, tt, :], res[slot][:, tt, :], ln2[:, tt, 0:1], rstd2[:, tt:tt + 1],
                                  ALU.subtract, ALU.mult).then_inc(out_ready, 1)

        HALVES = (range(TT // 2), range(TT // 2, TT))

        def ffn_block(b, b2, slot, first=False):
            for t in range(ET):
                if not (first and t == 0):
                    tile(b, t)
                if first and t == 1:
                    store_norm(CHUNKS // UNROLL - 1, UNROLL - 1)
                if not first:
                    if t == 1:
                        residual(b - 1, b2 - (1 - slot), 1 - slot)
                    if t in (2, 3):
                        norm_stats(b - 1, 1 - slot, HALVES[t - 2])
                    if t == 4:
                        norm_moments(b - 1)
                    if t in (6, 7):
                        norm_out(b - 1, 1 - slot, HALVES[t - 6])

        ffn_block(0, 0, 0, first=True)
        ffn_block(1, 0, 1)
        with dve.Fori(1, BLOCKS // 2) as i:
            for s in range(2):
                ffn_block(i * 2 + s, i, s)
        residual(BLOCKS - 1, BLOCKS // 2 - 1, 1)
        norm_stats(BLOCKS - 1, 1, range(TT))
        norm_moments(BLOCKS - 1)
        norm_out(BLOCKS - 1, 1, range(TT))

    @block.gpsimd
    def _(pool):
        pool.memset(causal[:], 1.0).then_inc(fill_done, 1)
        pool.memset(ident[:], 0.0).then_inc(fill_done, 1)
        pool.wait_ge(fill_done, 2)
        pool.affine_select(out=causal[:], in_=causal[:], compare_op=ALU.is_ge, fill=0.0, base=0, pattern=[[1, P]],
                           channel_multiplier=-1).then_inc(consts_ready, 1)
        pool.affine_select(out=ident[:], in_=ident[:], compare_op=ALU.not_equal, fill=1.0, base=0, pattern=[[1, P]],
                           channel_multiplier=-1).then_inc(consts_ready, 1)
        pool.wait_ge(consts_ready, 3)

        def rms_of(i, p):
            c, _, _, slot = at(i, p)
            col = slice(slot % 2, slot % 2 + 1)
            pool.wait_ge(ssq_ready, c + 1)
            carry(pool)
            s2 = ROW_SCALE * ROW_SCALE
            pool.tensor_scalar(ssq[:, col], ssq[:, col], 1.0 / (D * s2), RMS_EPS / s2, ALU.mult, ALU.add).then_inc(ms_ready, 1)
            pool.wait_ge(ms_ready, c + 1)
            pool.tensor_tensor(rms[:, col], ssq[:, col], minus_half[:, 0:1], ALU.pow).then_inc(rms_ready, 1)

        def weight_max(n):
            pool.wait_ge(wmax_ready, n + 1)
            pool.partition_all_reduce(wmax_all[:, n:n + 1], wmax[:, n:n + 1], P, bass.bass_isa.ReduceOp.max).then_inc(wmax_all_ready, 1)

        def rstd_of(c):
            pool.wait_ge(mv_ready, c + 1)
            carry(pool)
            pool.tensor_scalar(ln[:, 0, 1:2], ln[:, 0, 1:2], LN_EPS, None, ALU.add).then_inc(vareps_ready, 1)
            pool.wait_ge(vareps_ready, c + 1)
            pool.tensor_tensor(rstd[:, 0:1], ln[:, 0, 1:2], minus_half[:, 0:1], ALU.pow).then_inc(rstd_ready, 1)

        def step(i, p, last=False):
            c, _, _, _ = at(i, p)
            if not (last and p >= 2):
                rms_of(i, p + 2)
            rstd_of(c)

        rms_of(0, 0)
        weight_max(K_)
        rms_of(0, 1)
        weight_max(Q_)
        weight_max(G_)
        weight_max(V_)
        pool.wait_ge(whi_ready, OUT_ + 1)
        pool.tensor_tensor(w_out[1][:].rearrange("p k d -> p (k d)"), raw_weight(OUT_),
                           w_out[0][:].bitcast(F32).rearrange("p k d -> p (k d)"), ALU.subtract).then_inc(w_out_ready, 1)
        for p in range(UNROLL):
            step(0, p)
        pool.wait_ge(msum_ready, 1)
        pool.partition_all_reduce(msum_all[:, 0:MATS], msum[:, 0:MATS], P, bass.bass_isa.ReduceOp.add).then_inc(msum_all_ready, 1)
        with pool.Fori(1, CHUNKS // UNROLL - 1) as i:
            for p in range(UNROLL):
                step(i, p)
        for p in range(UNROLL):
            step(CHUNKS // UNROLL - 1, p, last=True)
        with pool.Fori(0, BLOCKS) as b:
            pool.wait_ge(mv2_ready, b + 1)
            carry(pool)
            pool.tensor_scalar(ln2[:, :, 1:2], ln2[:, :, 1:2], LN_EPS, None, ALU.add).then_inc(vareps2_ready, 1)
            pool.wait_ge(vareps2_ready, b + 1)
            pool.tensor_tensor(rstd2[:], ln2[:, :, 1], minus_half[:, 0:TT], ALU.pow).then_inc(rstd2_ready, 1)

    ctx.close()


def kernel(**inputs):
    import concourse.bacc as bacc
    from concourse.bass_utils import run_bass_kernel_spmd

    f = {n: np.asarray(a) for n, a in inputs.items()}

    def contraction_first(w):
        o, i = w.shape
        return w.T.reshape(i // P, P, o).transpose(1, 0, 2)

    w_attn = np.stack([contraction_first(f[f"L0_attn_W{n}"]).reshape(P, KT * D) for n in "kqgvp"])
    mats = [contraction_first(f[f"L0_ffn_W_{n}"]).reshape(P, KT, ET, P).transpose(0, 2, 1, 3).reshape(P, PER_MAT, PIECE)
            for n in ("up", "gate")] + [contraction_first(f["L0_ffn_W_down"]).reshape(P, PER_MAT, PIECE)]
    w_ffn = np.concatenate([m.transpose(1, 0, 2) for m in mats])
    arrays = {
        "x": np.ascontiguousarray(f["L0_attn_x"].reshape(CHUNKS, P, D)),
        "w_attn": np.ascontiguousarray(w_attn),
        "w_ffn": np.ascontiguousarray(w_ffn),
    }
    nc = bacc.Bacc("TRN2", target_bir_lowering=False, num_devices=1)
    args = [nc.dram_tensor(n, a.shape, mybir.dt.from_np(a.dtype), kind="ExternalInput").ap() for n, a in arrays.items()]
    out = nc.dram_tensor("out", (CHUNKS, P, D), F32, kind="ExternalOutput").ap()
    build(nc, *args, out)
    r = run_bass_kernel_spmd(nc, [arrays], core_ids=[0])
    return r.results[0]["out"].reshape(1, TOKENS, D)
```

```python
from contextlib import ExitStack

import numpy as np

import concourse.bass as bass
import concourse.mybir as mybir
from concourse.alu_op_type import AluOpType as ALU

ACT = mybir.ActivationFunctionType
AX = mybir.AxisListType
F32 = mybir.dt.float32
F32R = mybir.dt.float32r
F16 = mybir.dt.float16
I32 = mybir.dt.int32

P = 128
TOKENS, D, E = 4096, 512, 2048
KT = D // P
ET = E // P
CHUNKS = TOKENS // P
UNROLL = 4
BLOCK = 512
BLOCKS = TOKENS // BLOCK
TT = BLOCK // P
WARM_UP = 36
TAIL = 8

PIECE = 1024
MATS = 3
PIECES = MATS * D * E // (P * PIECE)
PER_MAT = PIECES // MATS
SUM_GROUPS = (3, 3, 2)
PER_STEP = sum(SUM_GROUPS)
SUM_STEPS = PIECES // PER_STEP
HALF = KT * D // 2

ROW_SCALE = 64.0
W_SCALE = 16384.0
H_SCALE = 8.0
RMS_EPS = float(np.finfo(np.float32).eps)
LN_EPS = 1e-5
QUANT_EPS = 1e-8
EXPONENT_BITS = 0x7F800000
K_, Q_, G_, V_, OUT_ = range(5)
UP, GATE = range(2)


def at(i, p):
    i = i + p // UNROLL
    p = p % UNROLL
    return i * UNROLL + p, i * 2 + p // 2, i, p


def build(nc, x, w_attn, w_ffn, out):
    ctx = ExitStack()
    phase_a = ExitStack()

    def sem(name):
        return ctx.enter_context(nc.semaphore(name))

    def sb(name, shape, dt, where=ctx):
        return where.enter_context(nc.sbuf_tensor(name, shape, dt))

    y_dram = nc.dram_tensor("y_dram", (CHUNKS, P, D), F32, kind="Internal").ap()
    yh_dram = nc.dram_tensor("yh_dram", (CHUNKS, P, D), F16, kind="Internal").ap()
    yl_dram = nc.dram_tensor("yl_dram", (CHUNKS, P, D), F16, kind="Internal").ap()

    codes = sb("codes", [P, MATS * ET, D], F16)
    yT = [sb(f"yT{b}", [P, 2, KT, BLOCK], F16) for b in range(2)]
    ffn_scale = sb("ffn_scale", [P, 16], F32)
    asum = sb("asum", [P, PIECES], F32)
    thr = sb("thr", [P, PIECES], F32)
    nthr = sb("nthr", [P, PIECES], F32)
    minus_half = sb("minus_half", [P, PER_MAT], F32)
    ln = sb("ln", [P, 2], F32)
    stats = sb("stats", [P, 6], F32)
    rstd = sb("rstd", [P, 2], F32)
    ln2 = sb("ln2", [P, TT, 2], F32)
    stats2 = sb("stats2", [P, TT, 6], F32)
    rstd2 = sb("rstd2", [P, TT], F32)

    w_proj = sb("w_proj", [P, 4, 2, KT, D], F16, phase_a)
    w_out = [sb(f"w_out_{n}", [P, KT, D], F32R, phase_a) for n in ("hi", "lo")]
    stage = sb("stage", [P, 4, PIECE], F32, phase_a)
    below = sb("below", [P, PIECE], F16, phase_a)
    kv = [sb(f"kv_{n}", [P, KT, D], F32R, phase_a) for n in ("hi", "lo")]
    x32 = sb("x32", [P, UNROLL, D], F32, phase_a)
    xn = sb("xn", [P, 2, D], F16, phase_a)
    xnT = sb("xnT", [P, 2, 2, KT, P], F16, phase_a)
    q32 = sb("q32", [P, KT // 2, 2, P], F32, phase_a)
    k32 = sb("k32", [P, D], F32, phase_a)
    v32 = sb("v32", [P, D], F32, phase_a)
    qT_parts = sb("qT_parts", [P, 2, KT, 2, P], F32R, phase_a)
    kT = [sb(f"kT_{n}", [P, KT, P], F32R, phase_a) for n in ("hi", "lo")]
    kN = [sb(f"kN_{n}", [P, D], F32R, phase_a) for n in ("hi", "lo")]
    vN = [sb(f"vN_{n}", [P, D], F32R, phase_a) for n in ("hi", "lo")]
    s_cross = sb("s_cross", [P, P], F32, phase_a)
    s_sum = sb("s_sum", [P, P], F32, phase_a)
    sT32 = sb("sT32", [P, P], F32, phase_a)
    sT = [sb(f"sT_{n}", [P, P], F32R, phase_a) for n in ("hi", "lo")]
    gate_t = sb("gate_t", [P, D], F32, phase_a)
    og32 = sb("og32", [P, D], F32, phase_a)
    ogT = [sb(f"ogT_{n}", [P, KT, P], F32R, phase_a) for n in ("hi", "lo")]
    u32 = sb("u32", [P, D], F32, phase_a)
    y32 = sb("y32", [P, D], F32, phase_a)
    yhl = sb("yhl", [P, 2, D], F16, phase_a)
    squares = sb("squares", [P, D], F16, phase_a)
    causal = sb("causal", [P, P], F32, phase_a)
    ident = sb("ident", [P, P], F32, phase_a)
    wmax_part = sb("wmax_part", [P, 4, 3], F32, phase_a)
    wmax = sb("wmax", [P, 4], F32, phase_a)
    wmax_all = sb("wmax_all", [P, 4], F32, phase_a)
    wpow = sb("wpow", [P, 4], F32, phase_a)
    winv = sb("winv", [P, 4], F32, phase_a)
    wscale = sb("wscale", [P, 4], F32, phase_a)
    wunscale = sb("wunscale", [P, 4], F32, phase_a)
    msum = sb("msum", [P, 4], F32, phase_a)
    msum_all = sb("msum_all", [P, 4], F32, phase_a)
    ssq = sb("ssq", [P, 2], F32, phase_a)
    rms = sb("rms", [P, 2], F32, phase_a)
    phase_a.close()

    def raw_weight(n, half=None):
        lo, hi = (8 * n, 8 * n + 8) if half is None else (8 * n + 4 * half, 8 * n + 4 * half + 4)
        return codes[:, lo:hi, :].bitcast(F32).rearrange("p a b -> p (a b)")

    def proj_half(n, part, half):
        return w_proj[:, n, part, KT // 2 * half:KT // 2 * (half + 1), :].rearrange("p k d -> p (k d)")

    res = [sb(f"res{b}", [P, TT, D], F32) for b in range(2)]
    silu_u = sb("silu_u", [P, 2, BLOCK], F32)
    h32 = sb("h32", [P, BLOCK], F32)
    hT = [sb(f"hT_{n}", [P, 2, BLOCK], F16) for n in ("hi", "lo")]
    hT_tail = [sb(f"hT_tail_{n}", [P, TAIL, BLOCK], F16) for n in ("hi", "lo")]

    def hidden(part, t, last):
        if last and t >= ET - TAIL:
            return hT_tail[part][:, t - (ET - TAIL), :]
        return hT[part][:, t % 2, :]

    state = [ctx.enter_context(nc.psum_tensor(f"state{t}", [P, D], F32)) for t in range(4)]
    work = [ctx.enter_context(nc.psum_tensor(f"work{t}", [P, D], F32)) for t in range(4)]

    TK, PK, SC, PG = range(4)
    OO, TOG, PV, WP = range(4, 8)
    PQ = 8

    def bank(p, use):
        return work[(18 * (p // 2) + 8 * (p % 2) + use) % 4]

    def bank_of(p, end):
        return (lambda use: state[{TK: 1, SC: 2, OO: 3, TOG: 0, WP: 1}[use]]) if end else (lambda use: bank(p, use))

    def q_half(part, half):
        return qT_parts[:, :, KT // 2 * half:KT // 2 * (half + 1), part, :].rearrange("p c k t -> p k c t")

    consts_ready = sem("consts_ready")
    passed = sem("passed")
    fill_done = sem("fill_done")
    w_loaded = [[sem(f"w_loaded{n}_{half}") for half in range(2)] for n in range(5)]
    wmax_part_ready, wsum_ready = sem("wmax_part_ready"), sem("wsum_ready")
    wmax_ready, wmax_all_ready = sem("wmax_ready"), sem("wmax_all_ready")
    small = sem("small")
    whi_ready, wlo_ready, w_out_ready = sem("whi_ready"), sem("wlo_ready"), sem("w_out_ready")
    piece_loaded = [sem(f"piece_loaded{s}") for s in range(4)]
    abs_done, msum_ready, msum_all_ready, thr_ready = (sem(n) for n in ("abs_done", "msum_ready", "msum_all_ready", "thr_ready"))
    below_ready, piece_coded = sem("below_ready"), sem("piece_coded")
    x_loaded = [sem(f"x_loaded{s}") for s in range(UNROLL)]
    ssq_ready, ms_ready, rms_ready = sem("ssq_ready"), sem("ms_ready"), sem("rms_ready")
    xhi_ready, xlo_ready = sem("xhi_ready"), sem("xlo_ready")
    xT_loaded = [sem(f"xT_loaded{s}") for s in range(2)]
    pk_done, pq_done, pg_done, pv_done = (sem(n) for n in ("pk_done", "pq_done", "pg_done", "pv_done"))
    k_ready, q_ready, g_ready, v_ready = (sem(n) for n in ("k_ready", "q_ready", "g_ready", "v_ready"))
    tk_done, tog_done = sem("tk_done"), sem("tog_done")
    qThi_ready, qTlo_ready = sem("qThi_ready"), sem("qTlo_ready")
    kThi_ready, kTlo_ready = sem("kThi_ready"), sem("kTlo_ready")
    ogThi_ready, ogTlo_ready = sem("ogThi_ready"), sem("ogTlo_ready")
    kNhi_ready, kNlo_ready = sem("kNhi_ready"), sem("kNlo_ready")
    vNhi_ready, vNlo_ready = sem("vNhi_ready"), sem("vNlo_ready")
    s_done, s_crossed, s_summed, s_masked, shi_ready, slo_ready = (
        sem(n) for n in ("s_done", "s_crossed", "s_summed", "s_masked", "shi_ready", "slo_ready"))
    o_done, og_ready = sem("o_done"), sem("og_ready")
    state_done, kvhi_ready, kvlo_ready = sem("state_done"), sem("kvhi_ready"), sem("kvlo_ready")
    wp_done, u_ready = sem("wp_done"), sem("u_ready")
    stats_ready, mv_ready, vareps_ready, rstd_ready = (sem(n) for n in ("stats_ready", "mv_ready", "vareps_ready", "rstd_ready"))
    y_ready, yhi_ready, ylo_ready = sem("y_ready"), sem("yhi_ready"), sem("ylo_ready")
    y_stored = sem("y_stored")
    yT_loaded = [sem(f"yT_loaded{b}") for b in range(2)]
    res_loaded = [sem(f"res_loaded{b}") for b in range(2)]
    up_done, gate_done, down_done = sem("up_done"), sem("gate_done"), sem("down_done")
    silu_ready, h_ready, hhi_ready, hlo_ready = (sem(n) for n in ("silu_ready", "h_ready", "hhi_ready", "hlo_ready"))
    z_read, stats2_ready, mv2_ready, vareps2_ready, rstd2_ready = (
        sem(n) for n in ("z_read", "stats2_ready", "mv2_ready", "vareps2_ready", "rstd2_ready"))
    out_ready = sem("out_ready")
    out_stored = [sem(f"out_stored{b}") for b in range(2)]

    block = ctx.enter_context(nc.Block())

    def carry(engine):
        engine.sem_inc(passed, 1)

    @block.sync
    def _(sp):
        def load_weight(n):
            for half in range(2):
                sp.dma_start(raw_weight(n, half), w_attn[n][:, HALF * half:HALF * (half + 1)]).then_inc(w_loaded[n][half], 16)

        def load_x(i, p):
            c, _, _, slot = at(i, p)
            sp.dma_start(x32[:, slot, :], x[c]).then_inc(x_loaded[slot], 16)

        def load_piece(t, slot):
            sp.dma_start(stage[:, slot, :], w_ffn[t]).then_inc(piece_loaded[slot], 16)

        def transpose_x(i, p):
            c, _, _, slot = at(i, p)
            sp.wait_ge(xhi_ready, c + 1)
            carry(sp)
            sp.dma_start(xnT[:, slot % 2, 0], xn[:, 0, :], transpose=True).then_inc(xT_loaded[slot % 2], 16)
            sp.wait_ge(xlo_ready, c + 1)
            carry(sp)
            sp.dma_start(xnT[:, slot % 2, 1], xn[:, 1, :], transpose=True).then_inc(xT_loaded[slot % 2], 16)

        def store_y(i, p):
            c, _, _, _ = at(i, p)
            sp.wait_ge(y_ready, c + 1)
            carry(sp)
            sp.dma_start(y_dram[c], y32[:]).then_inc(y_stored, 16)
            sp.wait_ge(yhi_ready, c + 1)
            carry(sp)
            sp.dma_start(yh_dram[c], yhl[:, 0, :]).then_inc(y_stored, 16)
            sp.wait_ge(ylo_ready, c + 1)
            carry(sp)
            sp.dma_start(yl_dram[c], yhl[:, 1, :]).then_inc(y_stored, 16)

        def load_transposed(b, slot):
            for part, src in enumerate((yh_dram, yl_dram)):
                sp.dma_start(yT[slot][:, part], src[bass.ts(b, TT)].rearrange("t p d -> (t p) d"),
                             transpose=True).then_inc(yT_loaded[slot], 16)

        def load_rows(b, slot):
            sp.dma_start(res[slot][:], y_dram[bass.ts(b, TT)].rearrange("t p d -> p t d")).then_inc(res_loaded[slot], 16)

        def store_block(b, slot):
            sp.wait_ge(out_ready, TT * (b + 1))
            carry(sp)
            sp.dma_start(out[bass.ts(b, TT)].rearrange("t p d -> p t d"), res[slot][:]).then_inc(out_stored[slot], 16)

        def step(i, p, first=False, summing=False, coding=False, last=False):
            c, pair, _, _ = at(i, p)
            if summing:
                for t in range(PER_STEP * p, PER_STEP * (p + 1)):
                    if t >= 4:
                        sp.wait_ge(abs_done, t - 3)
                    load_piece(t, t % 4)
            if coding:
                if p == 0:
                    sp.wait_ge(abs_done, PIECES)
                sp.wait_ge(piece_coded, c - UNROLL + 1)
                carry(sp)
                load_piece(c - UNROLL, p)
            if last and p == 1:
                sp.wait_ge(y_stored, 48 * (CHUNKS - UNROLL))
                load_transposed(0, 0)
                load_transposed(1, 1)
            if not first:
                store_y(i, p - 1)
            if not (last and p >= 2):
                if p % 2:
                    sp.wait_ge(pv_done, c + 1)
                else:
                    sp.wait_ge(pq_done, 2 * pair + 2)
                carry(sp)
                transpose_x(i, p + 2)
            if not last:
                sp.wait_ge(u_ready, c + 1)
                carry(sp)
                load_x(i, p + UNROLL)

        load_x(0, 0)
        load_weight(K_)
        load_x(0, 1)
        load_weight(Q_)
        transpose_x(0, 0)
        load_weight(G_)
        load_weight(V_)
        transpose_x(0, 1)
        load_weight(OUT_)
        load_x(0, 2)
        load_x(0, 3)
        for p in range(UNROLL):
            step(0, p, first=p == 0, summing=p < SUM_STEPS)
        with sp.Fori(1, CHUNKS // UNROLL - 1) as i:
            for p in range(UNROLL):
                step(i, p, coding=True)
        for p in range(UNROLL):
            step(CHUNKS // UNROLL - 1, p, last=True)
        store_y(CHUNKS // UNROLL - 1, UNROLL - 1)

        sp.wait_ge(y_stored, 48 * CHUNKS)
        load_rows(0, 0)
        load_rows(1, 1)
        with sp.Fori(0, BLOCKS // 2 - 1) as i:
            for s in range(2):
                b = i * 2 + s
                store_block(b, s)
                load_transposed(b + 2, s)
                sp.wait_ge(out_stored[s], 16 * (i + 1))
                carry(sp)
                load_rows(b + 2, s)
        store_block(BLOCKS - 2, 0)
        for tt in range(TT):
            sp.wait_ge(out_ready, TT * (BLOCKS - 1) + tt + 1)
            sp.dma_start(out[TT * (BLOCKS - 1) + tt], res[1][:, tt, :]).then_inc(out_stored[1], 16)
        sp.wait_ge(out_stored[0], 16 * (BLOCKS // 2))
        sp.wait_ge(out_stored[1], 16 * (BLOCKS // 2 - 1 + TT))

    @block.tensor
    def _(pe):
        PARTS = ((0, 0), (0, 1), (1, 0))

        def project(i, p, which, use, done, first=False):
            _, _, _, slot = at(i, p)
            dst = bank(p - 1, use)
            for k in range(KT):
                if first and k % (KT // 2) == 0:
                    pe.wait_ge(wlo_ready, 2 * which + 1 + k // (KT // 2))
                for n, (a, b) in enumerate(PARTS):
                    mm = pe.matmul(dst[:], xnT[:, slot % 2, a, k, :], w_proj[:, which, b, k, :],
                                   start=n == 0 and k == 0, stop=n == 2 and k == KT - 1)
            mm.then_inc(done, 1)

        def transposes(dst, src, done):
            for k in range(KT):
                mm = pe.transpose(dst[:, k * P:(k + 1) * P], src[:, k * P:(k + 1) * P], ident[:])
            mm.then_inc(done, 1)

        def split_product(dst, lhs, rhs, start, stop):
            for n, (a, b) in enumerate(PARTS):
                mm = pe.matmul(dst, lhs[a], rhs[b], start=start and n == 0, stop=stop and n == 2, skip_group_check=True)
            return mm

        def tiles(t, n):
            return [t[0][:, n, :], t[1][:, n, :]]

        def project_q(i, p, done, first=False):
            for m in range(KT):
                dst = bank(p - 1, PQ + m // 2)[:, (m % 2) * 2 * P:(m % 2 + 1) * 2 * P]
                if first and m == KT // 2:
                    pe.wait_ge(k_ready, 1)
                for k in range(KT):
                    if first and m == 0 and k % (KT // 2) == 0:
                        pe.wait_ge(wlo_ready, 2 * Q_ + 1 + k // (KT // 2))
                    for n, (b, a) in enumerate(PARTS):
                        mm = pe.matmul(dst, w_proj[:, Q_, b, k, m * P:(m + 1) * P], xnT[:, :, a, k, :],
                                       start=n == 0 and k == 0, stop=n == 2 and k == KT - 1, skip_group_check=True)
                if m % 2:
                    mm.then_inc(done, 1)

        def step(i, p, first=False, last=False):
            c, pair, _, _ = at(i, p)
            odd = p % 2 == 1
            end = last and p == UNROLL - 1
            my = bank_of(p, end)
            if end:
                pe.wait_ge(kvlo_ready, KT * c)
            elif not odd:
                pe.wait_ge(v_ready, c + 1)
            pe.wait_ge(k_ready, c + 1)
            transposes(my(TK), k32, tk_done)
            if end:
                pe.wait_ge(v_ready, c + 1)
                pe.wait_ge(yT_loaded[0], 32)
                expand(0, 0, 0, UP)
            else:
                if first:
                    pe.wait_ge(g_ready, 1)
                elif not odd:
                    pe.wait_ge(u_ready, c)
                _, c2, _, slot = at(i, p + 1)
                pe.wait_ge(xT_loaded[slot % 2], 32 * (c2 + 1))
                project(i, p + 1, K_, PK, pk_done)
            pe.wait_ge(qTlo_ready, 2 * pair + 2)
            pe.wait_ge(kTlo_ready, c + 1)
            if odd and not end:
                pe.wait_ge(v_ready, c + 1)
            for k in range(KT):
                for part in range(2):
                    mm = pe.matmul(my(SC)[:, 0:2 * P], kT[part][:, k, :], qT_parts[:, p % 2, k].rearrange("p a t -> p (a t)"),
                                   start=k == 0 and part == 0, stop=k == KT - 1 and part == 1)
            mm.then_inc(s_done, 1)
            if end:
                pe.wait_ge(ogTlo_ready, c)
                pe.wait_ge(piece_coded, UNROLL + PIECES)
                expand(0, 0, 0, GATE)
            else:
                if odd:
                    pe.wait_ge(u_ready, c)
                project(i, p + 1, G_, PG, pg_done)
            pe.wait_ge(slo_ready, c + 1)
            pe.wait_ge(vNlo_ready, c + 1)
            mm = split_product(my(OO)[:], [sT[0][:], sT[1][:]], [vN[0][:], vN[1][:]], True, first)
            if not first:
                pe.wait_ge(kvlo_ready, KT * c)
                for k in range(KT):
                    mm = split_product(my(OO)[:], [qT_parts[:, p % 2, k, part, :] for part in range(2)], tiles(kv, k),
                                       False, k == KT - 1)
            mm.then_inc(o_done, 1)
            if end:
                pe.wait_ge(u_ready, c)
                expand(0, 0, 1, UP)
            else:
                pe.wait_ge(kNlo_ready, c + 1)
                for t in range(KT):
                    split_product(state[t][:], [part[:, t * P:(t + 1) * P] for part in kN], [vN[0][:], vN[1][:]],
                                  first, True).then_inc(state_done, 1)
                pe.wait_ge(k_ready, c + 2)
            pe.wait_ge(og_ready, c + 1)
            transposes(my(TOG), og32, tog_done)
            if end:
                expand(0, 0, 1, GATE)
            else:
                project(i, p + 1, V_, PV, pv_done)
                pe.wait_ge(g_ready, c + 2)
            pe.wait_ge(ogTlo_ready, c + 1)
            if first:
                pe.wait_ge(w_out_ready, 1)
            for k in range(KT):
                mm = split_product(my(WP)[:], tiles(ogT, k), tiles(w_out, k), k == 0, k == KT - 1)
            mm.then_inc(wp_done, 1)
            if odd and not end:
                _, c2, _, slot = at(i, p + 2)
                pe.wait_ge(xT_loaded[slot % 2], 32 * (c2 + 1))
                project_q(i, p + 1, pq_done)

        def expand(b, slot, t, which):
            dst, done = (work[t % 2], up_done) if which == UP else (work[2 + t % 2], gate_done)
            for k in range(KT):
                for part in range(2):
                    mm = pe.matmul(dst[:], codes[:, which * ET + t, k * P:(k + 1) * P], yT[slot][:, part, k, :],
                                   start=part == 0 and k == 0, stop=part == 1 and k == KT - 1)
            mm.then_inc(done, 1)

        pe.wait_ge(consts_ready, 3)
        pe.wait_ge(w_loaded[K_][1], 16)
        for _ in range(WARM_UP):
            pe.transpose(state[0][:, 0:P], ident[:], ident[:])
        pe.wait_ge(xT_loaded[0], 32)
        project(0, 0, K_, PK, pk_done, first=True)
        pe.wait_ge(xT_loaded[1], 32)
        project_q(0, 0, pq_done, first=True)
        project(0, 0, G_, PG, pg_done, first=True)
        project(0, 0, V_, PV, pv_done, first=True)
        for p in range(UNROLL):
            step(0, p, first=p == 0)
        with pe.Fori(1, CHUNKS // UNROLL - 1) as i:
            for p in range(UNROLL):
                step(i, p)
        for p in range(UNROLL):
            step(CHUNKS // UNROLL - 1, p, last=True)

        def contract(b, t, tt, last=False):
            for part in range(2):
                mm = pe.matmul(state[tt][:], hidden(part, t, last)[:, tt * P:(tt + 1) * P], codes[:, 2 * ET + t, :],
                               start=t == 0 and part == 0, stop=t == ET - 1 and part == 1, skip_group_check=True)
            mm.then_inc(down_done, 1)

        def ffn_block(b, b2, slot, last=False):
            for t in range(ET):
                ahead = (t + 2) % ET
                if not (last and ahead < 2):
                    nb, nslot = (b, slot) if t < ET - 2 else (b + 1, 1 - slot)
                    if t == ET - 2:
                        pe.wait_ge(yT_loaded[1 - slot], 32 * (b2 + slot + 1))
                    pe.wait_ge(h_ready, nb * ET + ahead + 1)
                    expand(nb, nslot, ahead, UP)
                    expand(nb, nslot, ahead, GATE)
                if not (last and t >= ET - TAIL):
                    pe.wait_ge(hlo_ready, b * ET + t + 1)
                    for tt in range(TT):
                        if t == 0:
                            pe.wait_ge(z_read, TT * b + tt + 1)
                        contract(b, t, tt)
            if last:
                for tt in range(TT):
                    for t in range(ET - TAIL, ET):
                        if tt == 0:
                            pe.wait_ge(hlo_ready, b * ET + t + 1)
                        contract(b, t, tt, last=True)

        with pe.Fori(0, BLOCKS // 2 - 1) as i:
            for s in range(2):
                ffn_block(i * 2 + s, i, s)
        ffn_block(BLOCKS - 2, BLOCKS // 2 - 1, 0)
        ffn_block(BLOCKS - 1, BLOCKS // 2 - 1, 1, last=True)

    @block.scalar
    def _(act):
        def square_x(i, p):
            c, _, c4, slot = at(i, p)
            act.wait_ge(x_loaded[slot], 16 * (c4 + 1))
            act.wait_ge(ssq_ready, c)
            act.activation(squares[:], x32[:, slot, :], ACT.Square, accum_out=ssq[:, slot % 2:slot % 2 + 1]).then_inc(ssq_ready, 1)

        def norm_x(i, p):
            c, c2, _, slot = at(i, p)
            act.wait_ge(rms_ready, c + 1)
            if not (isinstance(c, int) and c == 0):
                pc, pc2, _, pslot = at(i, p - 1)
                act.wait_ge(xT_loaded[pslot % 2], 32 * (pc2 + 1))
            act.activation(xn[:, 0, :], x32[:, slot, :], ACT.Copy, scale=rms[:, slot % 2:slot % 2 + 1]).then_inc(xhi_ready, 1)

        def project_k(c, p):
            act.wait_ge(pk_done, c + 1)
            act.wait_ge(kNlo_ready, c)
            act.activation(k32[:], bank(p - 1, PK)[:], ACT.Silu, scale=wunscale[:, K_:K_ + 1]).then_inc(k_ready, 1)

        def project_q(i, p, halves=range(2)):
            _, pair, _, _ = at(i, p)
            for half in halves:
                act.wait_ge(pq_done, 2 * pair + half + 1)
                if half or not (isinstance(pair, int) and pair == 0):
                    act.wait_ge(qTlo_ready, 2 * pair + half)
                act.activation(q32[:].rearrange("p k c t -> p (k c t)"), bank(p - 1, PQ + half)[:], ACT.Silu,
                               scale=wunscale[:, Q_:Q_ + 1]).then_inc(q_ready, 1)
                act.wait_ge(q_ready, 2 * pair + half + 1)
                act.activation(q_half(0, half), q32[:], ACT.Copy).then_inc(qThi_ready, 1)

        def project_g(c, p):
            act.wait_ge(pg_done, c + 1)
            act.wait_ge(og_ready, c)
            act.activation(gate_t[:], bank(p - 1, PG)[:], ACT.Tanh, scale=wunscale[:, G_:G_ + 1]).then_inc(g_ready, 1)

        def project_v(c, p):
            act.wait_ge(pv_done, c + 1)
            act.wait_ge(vNlo_ready, c)
            act.activation(v32[:], bank(p - 1, PV)[:], ACT.Silu, scale=wunscale[:, V_:V_ + 1]).then_inc(v_ready, 1)

        def sum_pieces(p, group):
            start = PER_STEP * p + sum(SUM_GROUPS[:group])
            for t in range(start, start + SUM_GROUPS[group]):
                act.wait_ge(piece_loaded[t % 4], 16 * (t // 4 + 1))
                act.wait_ge(abs_done, t)
                act.activation(below[:], stage[:, t % 4, :], ACT.Abs, accum_out=asum[:, t:t + 1]).then_inc(abs_done, 1)

        def step(i, p, summing=False, last=False):
            c, _, _, _ = at(i, p)
            nxt = not (last and p == UNROLL - 1)
            my = bank_of(p, not nxt)
            act.wait_ge(tk_done, c + 1)
            act.activation(kT[0][:], my(TK)[:].rearrange("p (k t) -> p k t", k=KT), ACT.Copy).then_inc(kThi_ready, 1)
            if not (last and p >= 2):
                square_x(i, p + 2)
            if summing:
                sum_pieces(p, 0)
            if nxt:
                project_k(c + 1, p + 1)
            if not (last and p >= 2):
                norm_x(i, p + 2)
            if summing:
                sum_pieces(p, 1)
            act.wait_ge(tog_done, c + 1)
            act.activation(ogT[0][:], my(TOG)[:].rearrange("p (k t) -> p k t", k=KT), ACT.Copy).then_inc(ogThi_ready, 1)
            if nxt:
                project_g(c + 1, p + 1)
                for t in range(KT):
                    act.wait_ge(state_done, KT * c + t + 1)
                    act.activation(kv[0][:, t, :], state[t][:], ACT.Copy).then_inc(kvhi_ready, 1)
                project_v(c + 1, p + 1)
                if summing:
                    sum_pieces(p, 2)
                if p % 2:
                    project_q(i, p + 1)

        def split_weight(n):
            for half in range(2):
                act.wait_ge(w_loaded[n][half], 16)
            if n < OUT_:
                act.wait_ge(small, 4 * n + 3)
                for half in range(2):
                    act.activation(proj_half(n, 0, half), raw_weight(n, half), ACT.Copy,
                                   scale=wscale[:, n:n + 1]).then_inc(whi_ready, 1)
            else:
                act.activation(w_out[0][:].rearrange("p k d -> p (k d)"), raw_weight(n), ACT.Copy).then_inc(whi_ready, 1)

        def sum_weight(n, half, k):
            act.wait_ge(w_loaded[n][half], 16)
            act.wait_ge(wsum_ready, k)
            act.activation(below[:], raw_weight(n, half), ACT.Abs, accum_out=wmax_part[:, n, half:half + 1]).then_inc(wsum_ready, 1)

        square_x(0, 0)
        norm_x(0, 0)
        act.wait_ge(wmax_part_ready, 1)
        sum_weight(K_, 1, 0)
        square_x(0, 1)
        split_weight(K_)
        norm_x(0, 1)
        sum_weight(G_, 0, 1)
        split_weight(Q_)
        project_k(0, 0)
        sum_weight(V_, 0, 2)
        split_weight(G_)
        project_q(0, 0, [0])
        split_weight(V_)
        project_q(0, 0, [1])
        project_g(0, 0)
        project_v(0, 0)
        split_weight(OUT_)
        act.wait_ge(wsum_ready, 3)
        for p in range(UNROLL):
            step(0, p, summing=p < SUM_STEPS)
        with act.Fori(1, CHUNKS // UNROLL - 1) as i:
            for p in range(UNROLL):
                step(i, p)
        for p in range(UNROLL):
            step(CHUNKS // UNROLL - 1, p, last=True)

        act.wait_ge(small, 26)

        def tile(b, t, last=False):
            n = b * ET + t
            act.wait_ge(up_done, n + 1)
            act.wait_ge(h_ready, n + 1)
            act.activation(silu_u[:, t % 2, :], work[t % 2][:], ACT.Silu, scale=ffn_scale[:, 0:1]).then_inc(silu_ready, 1)
            act.wait_ge(h_ready, n + 3)
            if not (isinstance(n, int) and n < 2) and not (last and t >= ET - TAIL):
                act.wait_ge(down_done, TT * (n - 1))
            act.activation(hidden(0, t, last), h32[:], ACT.Copy).then_inc(hhi_ready, 1)

        for t in range(ET):
            tile(0, t)
        with act.Fori(1, BLOCKS - 1) as b:
            for t in range(ET):
                tile(b, t)
        for t in range(ET):
            tile(BLOCKS - 1, t, last=True)

    @block.vector
    def _(dve):
        def small_done(n):
            dve.wait_ge(small, n)

        def largest_weight(n, half):
            dve.wait_ge(w_loaded[n][half], 16)
            dve.tensor_reduce(wmax_part[:, n, half:half + 1], raw_weight(n, half), AX.X, ALU.max,
                              apply_absolute_value=True).then_inc(wmax_part_ready, 1)

        def bound_of_weight(n, largest, sums):
            dve.wait_ge(wmax_part_ready, 1 + largest)
            if sums:
                dve.wait_ge(wsum_ready, sums)
            dve.tensor_reduce(wmax[:, n:n + 1], wmax_part[:, n, :], AX.X, ALU.max).then_inc(wmax_ready, 1)

        def scale_of_weight(n):
            col = slice(n, n + 1)
            dve.wait_ge(wmax_all_ready, n + 1)
            dve.tensor_scalar(wpow[:, col].bitcast(I32), wmax_all[:, col].bitcast(I32), EXPONENT_BITS, None,
                              ALU.bitwise_and).then_inc(small, 1)
            small_done(4 * n + 1)
            dve.reciprocal(winv[:, col], wpow[:, col]).then_inc(small, 1)
            small_done(4 * n + 2)
            dve.tensor_scalar(wscale[:, col], winv[:, col], W_SCALE, None, ALU.mult).then_inc(small, 1)
            dve.tensor_scalar(wunscale[:, col], wpow[:, col], (0.5 if n == G_ else 1.0) / (W_SCALE * ROW_SCALE), None,
                              ALU.mult).then_inc(small, 1)

        def split_weight(n, half):
            dve.wait_ge(whi_ready, 2 * n + half + 1)
            dve.scalar_tensor_tensor(out=proj_half(n, 1, half), in0=raw_weight(n, half), scalar=wscale[:, n:n + 1],
                                     in1=proj_half(n, 0, half), op0=ALU.mult, op1=ALU.subtract).then_inc(wlo_ready, 1)

        def norm_x(i, p):
            c, _, _, slot = at(i, p)
            dve.wait_ge(xhi_ready, c + 1)
            dve.scalar_tensor_tensor(out=xn[:, 1, :], in0=x32[:, slot, :], scalar=rms[:, slot % 2:slot % 2 + 1],
                                     in1=xn[:, 0, :], op0=ALU.mult, op1=ALU.subtract).then_inc(xlo_ready, 1)

        def split_k(c):
            dve.wait_ge(k_ready, c + 1)
            dve.tensor_copy(kN[0][:], k32[:]).then_inc(kNhi_ready, 1)
            dve.wait_ge(kNhi_ready, c + 1)
            dve.tensor_tensor(kN[1][:], k32[:], kN[0][:].bitcast(F32), ALU.subtract).then_inc(kNlo_ready, 1)

        def split_v(c):
            dve.wait_ge(v_ready, c + 1)
            dve.tensor_copy(vN[0][:], v32[:]).then_inc(vNhi_ready, 1)
            dve.wait_ge(vNhi_ready, c + 1)
            dve.tensor_tensor(vN[1][:], v32[:], vN[0][:].bitcast(F32), ALU.subtract).then_inc(vNlo_ready, 1)

        def low_of(dst, src, hi, hi_ready, value, done):
            dve.wait_ge(hi_ready, value)
            dve.tensor_tensor(dst, src, hi.bitcast(F32), ALU.subtract).then_inc(done, 1)

        def split_q(i, p, halves=range(2)):
            _, pair, _, _ = at(i, p)
            for half in halves:
                low_of(q_half(1, half), q32[:], q_half(0, half), qThi_ready, 2 * pair + half + 1, qTlo_ready)

        def store_norm(i, p):
            c, _, _, _ = at(i, p)
            dve.wait_ge(rstd_ready, c + 1)
            dve.wait_ge(y_stored, 48 * c)
            dve.tensor_scalar(y32[:], u32[:], ln[:, 0:1], rstd[:, 0:1], ALU.subtract, ALU.mult).then_inc(y_ready, 1)
            dve.wait_ge(y_ready, c + 1)
            dve.tensor_scalar(yhl[:, 0, :], y32[:], ROW_SCALE, None, ALU.mult).then_inc(yhi_ready, 1)
            dve.wait_ge(yhi_ready, c + 1)
            dve.scalar_tensor_tensor(out=yhl[:, 1, :], in0=y32[:], scalar=ROW_SCALE, in1=yhl[:, 0, :],
                                     op0=ALU.mult, op1=ALU.subtract).then_inc(ylo_ready, 1)

        def tile(b, t, last=False):
            n = b * ET + t
            dve.wait_ge(silu_ready, n + 1)
            dve.wait_ge(gate_done, n + 1)
            dve.wait_ge(hlo_ready, n)
            dve.scalar_tensor_tensor(out=h32[:], in0=silu_u[:, t % 2, :], scalar=ffn_scale[:, 3:4], in1=work[2 + t % 2][:],
                                     op0=ALU.mult, op1=ALU.mult).then_inc(h_ready, 1)
            dve.wait_ge(hhi_ready, n + 1)
            dve.tensor_tensor(hidden(1, t, last), h32[:], hidden(0, t, last), ALU.subtract).then_inc(hlo_ready, 1)

        def step(i, p, first=False, scales=False, coding=False, last=False):
            c, _, _, _ = at(i, p)
            nxt = not (last and p == UNROLL - 1)
            my = bank_of(p, not nxt)
            low_of(kT[1][:], my(TK)[:].rearrange("p (k t) -> p k t", k=KT), kT[0][:], kThi_ready, c + 1, kTlo_ready)
            if p % 2:
                split_v(c)
            dve.wait_ge(s_done, c + 1)
            dve.tensor_copy(s_cross[:], my(SC)[:, P:2 * P]).then_inc(s_crossed, 1)
            dve.wait_ge(s_crossed, c + 1)
            dve.tensor_tensor(s_sum[:], my(SC)[:, 0:P], s_cross[:], ALU.add).then_inc(s_summed, 1)
            dve.wait_ge(s_summed, c + 1)
            dve.tensor_tensor(sT32[:], s_sum[:], causal[:], ALU.mult).then_inc(s_masked, 1)
            dve.wait_ge(s_masked, c + 1)
            dve.tensor_copy(sT[0][:], sT32[:]).then_inc(shi_ready, 1)
            dve.wait_ge(shi_ready, c + 1)
            dve.tensor_tensor(sT[1][:], sT32[:], sT[0][:].bitcast(F32), ALU.subtract).then_inc(slo_ready, 1)
            if not first:
                store_norm(i, p - 1)
            if scales:
                thresholds()
            if coding:
                dve.wait_ge(piece_loaded[p], 16 * (PIECES // UNROLL + i))
                if p == 0:
                    dve.wait_ge(thr_ready, 1)
                dve.wait_ge(piece_coded, c)
                piece = c - UNROLL
                dve.tensor_scalar(below[:], stage[:, p, :], nthr[:, bass.ts(piece, 1)], None, ALU.is_lt).then_inc(below_ready, 1)
                dve.wait_ge(below_ready, piece + 1)
                dve.scalar_tensor_tensor(out=codes[:, bass.ts(piece, 2), :].rearrange("p a b -> p (a b)"),
                                         in0=stage[:, p, :], scalar=thr[:, bass.ts(piece, 1)], in1=below[:],
                                         op0=ALU.is_gt, op1=ALU.subtract).then_inc(piece_coded, 1)
            if not (last and p >= 2):
                norm_x(i, p + 2)
            dve.wait_ge(o_done, c + 1)
            dve.scalar_tensor_tensor(out=og32[:], in0=gate_t[:], scalar=1.0, in1=my(OO)[:],
                                     op0=ALU.add, op1=ALU.mult).then_inc(og_ready, 1)
            low_of(ogT[1][:], my(TOG)[:].rearrange("p (k t) -> p k t", k=KT), ogT[0][:], ogThi_ready, c + 1, ogTlo_ready)
            if nxt:
                for t in range(KT):
                    low_of(kv[1][:, t, :], state[t][:], kv[0][:, t, :], kvhi_ready, KT * c + t + 1, kvlo_ready)
                split_k(c + 1)
            if not nxt:
                tile(0, 0)
            dve.wait_ge(wp_done, c + 1)
            dve.scalar_tensor_tensor(out=u32[:], in0=my(WP)[:], scalar=0.5, in1=x32[:, p % UNROLL, :],
                                     op0=ALU.mult, op1=ALU.add).then_inc(u_ready, 1)
            dve.wait_ge(u_ready, c + 1)
            dve.bn_stats(stats[:], u32[:]).then_inc(stats_ready, 1)
            dve.wait_ge(stats_ready, c + 1)
            carry(dve)
            dve.bn_aggr(ln[:], stats[:]).then_inc(mv_ready, 1)
            if nxt and p % 2:
                split_v(c + 1)
                split_q(i, p + 1)

        def sum_of_weights():
            dve.wait_ge(abs_done, PIECES)
            dve.tensor_reduce(msum[:, 0:MATS], asum[:].rearrange("p (m j) -> p m j", m=MATS), AX.X, ALU.add).then_inc(msum_ready, 1)

        def thresholds():
            dve.wait_ge(msum_all_ready, 1)
            dve.tensor_scalar(ffn_scale[:, 0:MATS], msum_all[:, 0:MATS], 1.0 / (D * E), QUANT_EPS, ALU.mult, ALU.add).then_inc(small, 1)
            small_done(17)
            for m in range(MATS):
                dve.tensor_scalar(nthr[:, m * PER_MAT:(m + 1) * PER_MAT], minus_half[:], ffn_scale[:, m:m + 1], None,
                                  ALU.mult).then_inc(small, 1)
            small_done(20)
            dve.tensor_scalar(thr[:], nthr[:], -1.0, None, ALU.mult).then_inc(thr_ready, 1)
            dve.reciprocal(ffn_scale[:, 5:6], ffn_scale[:, 0:1]).then_inc(small, 1)
            dve.tensor_tensor(ffn_scale[:, 6:7], ffn_scale[:, 0:1], ffn_scale[:, 1:2], ALU.mult).then_inc(small, 1)
            small_done(22)
            dve.tensor_scalar(ffn_scale[:, 3:4], ffn_scale[:, 5:6], 1.0 / (H_SCALE * ROW_SCALE), None, ALU.mult).then_inc(small, 1)
            dve.tensor_tensor(ffn_scale[:, 7:8], ffn_scale[:, 6:7], ffn_scale[:, 2:3], ALU.mult).then_inc(small, 1)
            small_done(24)
            dve.tensor_scalar(ffn_scale[:, 4:5], ffn_scale[:, 7:8], H_SCALE, None, ALU.mult).then_inc(small, 1)
            dve.tensor_scalar(ffn_scale[:, 0:1], ffn_scale[:, 0:1], 1.0 / ROW_SCALE, None, ALU.mult).then_inc(small, 1)

        dve.sem_inc(h_ready, 2)
        dve.sem_inc(piece_coded, UNROLL)
        dve.memset(minus_half[:], -0.5).then_inc(consts_ready, 1)
        dve.memset(wmax_part[:], 2.0 ** -100).then_inc(wmax_part_ready, 1)
        dve.wait_ge(wmax_part_ready, 1)
        largest_weight(K_, 0)
        norm_x(0, 0)
        bound_of_weight(K_, 1, 1)
        scale_of_weight(K_)
        largest_weight(Q_, 0)
        largest_weight(Q_, 1)
        bound_of_weight(Q_, 3, 0)
        split_weight(K_, 0)
        scale_of_weight(Q_)
        norm_x(0, 1)
        split_weight(K_, 1)
        split_weight(Q_, 0)
        split_weight(Q_, 1)
        largest_weight(G_, 1)
        bound_of_weight(G_, 4, 2)
        largest_weight(V_, 1)
        scale_of_weight(G_)
        bound_of_weight(V_, 5, 3)
        scale_of_weight(V_)
        split_weight(G_, 0)
        split_weight(G_, 1)
        split_q(0, 0, [0])
        split_weight(V_, 0)
        split_weight(V_, 1)
        split_k(0)
        split_q(0, 0, [1])
        split_v(0)
        dve.wait_ge(consts_ready, 3)
        for p in range(UNROLL):
            step(0, p, first=p == 0, scales=p == SUM_STEPS)
            if p == SUM_STEPS - 1:
                sum_of_weights()
        with dve.Fori(1, CHUNKS // UNROLL - 1) as i:
            for p in range(UNROLL):
                step(i, p, coding=True)
        for p in range(UNROLL):
            step(CHUNKS // UNROLL - 1, p, last=True)

        dve.sem_inc(z_read, TT)

        def residual(b, b2, slot):
            dve.wait_ge(res_loaded[slot], 16 * (b2 + 1))
            for tt in range(TT):
                dve.wait_ge(down_done, TT * (ET * b + ET - 1) + tt + 1)
                dve.scalar_tensor_tensor(out=res[slot][:, tt, :], in0=state[tt][:], scalar=ffn_scale[:, 4:5],
                                         in1=res[slot][:, tt, :], op0=ALU.mult, op1=ALU.add).then_inc(z_read, 1)

        def norm_stats(b, slot, tts):
            for tt in tts:
                dve.wait_ge(z_read, TT * (b + 1) + tt + 1)
                dve.bn_stats(stats2[:, tt, :], res[slot][:, tt, :]).then_inc(stats2_ready, 1)

        def norm_moments(b):
            for tt in range(TT):
                dve.wait_ge(stats2_ready, TT * b + tt + 1)
                carry(dve)
                bn = dve.bn_aggr(ln2[:, tt, :], stats2[:, tt, :])
            bn.then_inc(mv2_ready, 1)

        def norm_out(b, slot, tts):
            dve.wait_ge(rstd2_ready, b + 1)
            for tt in tts:
                dve.tensor_scalar(res[slot][:, tt, :], res[slot][:, tt, :], ln2[:, tt, 0:1], rstd2[:, tt:tt + 1],
                                  ALU.subtract, ALU.mult).then_inc(out_ready, 1)

        HALVES = (range(TT // 2), range(TT // 2, TT))

        def ffn_block(b, b2, slot, first=False, last=False):
            for t in range(ET):
                if not (first and t == 0):
                    tile(b, t, last)
                if first and t == 1:
                    store_norm(CHUNKS // UNROLL - 1, UNROLL - 1)
                if not first:
                    if t == 1:
                        residual(b - 1, b2 - (1 - slot), 1 - slot)
                    if t in (2, 3):
                        norm_stats(b - 1, 1 - slot, HALVES[t - 2])
                    if t == 4:
                        norm_moments(b - 1)
                    if t in (6, 7):
                        norm_out(b - 1, 1 - slot, HALVES[t - 6])

        ffn_block(0, 0, 0, first=True)
        ffn_block(1, 0, 1)
        with dve.Fori(1, BLOCKS // 2 - 1) as i:
            for s in range(2):
                ffn_block(i * 2 + s, i, s)
        ffn_block(BLOCKS - 2, BLOCKS // 2 - 1, 0)
        ffn_block(BLOCKS - 1, BLOCKS // 2 - 1, 1, last=True)

        b = BLOCKS - 1

        def last_norm_out(tt):
            dve.wait_ge(rstd2_ready, b + tt + 1)
            dve.tensor_scalar(res[1][:, tt, :], res[1][:, tt, :], ln2[:, tt, 0:1], rstd2[:, tt:tt + 1],
                              ALU.subtract, ALU.mult).then_inc(out_ready, 1)

        dve.wait_ge(res_loaded[1], 16 * (BLOCKS // 2))
        for tt in range(TT):
            if tt >= 1:
                last_norm_out(tt - 1)
            dve.wait_ge(down_done, TT * (ET * b + ET - TAIL) + TAIL * (tt + 1))
            dve.scalar_tensor_tensor(out=res[1][:, tt, :], in0=state[tt][:], scalar=ffn_scale[:, 4:5],
                                     in1=res[1][:, tt, :], op0=ALU.mult, op1=ALU.add).then_inc(z_read, 1)
            dve.wait_ge(z_read, TT * (b + 1) + tt + 1)
            dve.bn_stats(stats2[:, tt, :], res[1][:, tt, :]).then_inc(stats2_ready, 1)
            dve.wait_ge(stats2_ready, TT * b + tt + 1)
            dve.bn_aggr(ln2[:, tt, :], stats2[:, tt, :]).then_inc(mv2_ready, 1)
        last_norm_out(TT - 1)

    @block.gpsimd
    def _(pool):
        pool.memset(causal[:], 1.0).then_inc(fill_done, 1)
        pool.memset(ident[:], 0.0).then_inc(fill_done, 1)
        pool.wait_ge(fill_done, 2)
        pool.affine_select(out=causal[:], in_=causal[:], compare_op=ALU.is_ge, fill=0.0, base=0, pattern=[[1, P]],
                           channel_multiplier=-1).then_inc(consts_ready, 1)
        pool.affine_select(out=ident[:], in_=ident[:], compare_op=ALU.not_equal, fill=1.0, base=0, pattern=[[1, P]],
                           channel_multiplier=-1).then_inc(consts_ready, 1)
        pool.wait_ge(consts_ready, 3)

        def rms_of(i, p):
            c, _, _, slot = at(i, p)
            col = slice(slot % 2, slot % 2 + 1)
            pool.wait_ge(ssq_ready, c + 1)
            carry(pool)
            s2 = ROW_SCALE * ROW_SCALE
            pool.tensor_scalar(ssq[:, col], ssq[:, col], 1.0 / (D * s2), RMS_EPS / s2, ALU.mult, ALU.add).then_inc(ms_ready, 1)
            pool.wait_ge(ms_ready, c + 1)
            pool.tensor_tensor(rms[:, col], ssq[:, col], minus_half[:, 0:1], ALU.pow).then_inc(rms_ready, 1)

        def weight_max(n):
            pool.wait_ge(wmax_ready, n + 1)
            pool.partition_all_reduce(wmax_all[:, n:n + 1], wmax[:, n:n + 1], P, bass.bass_isa.ReduceOp.max).then_inc(wmax_all_ready, 1)

        def rstd_of(c):
            pool.wait_ge(mv_ready, c + 1)
            carry(pool)
            pool.tensor_scalar(ln[:, 1:2], ln[:, 1:2], LN_EPS, None, ALU.add).then_inc(vareps_ready, 1)
            pool.wait_ge(vareps_ready, c + 1)
            pool.tensor_tensor(rstd[:, 0:1], ln[:, 1:2], minus_half[:, 0:1], ALU.pow).then_inc(rstd_ready, 1)

        def step(i, p, last=False):
            c, _, _, _ = at(i, p)
            if not (last and p >= 2):
                rms_of(i, p + 2)
            rstd_of(c)

        rms_of(0, 0)
        weight_max(K_)
        rms_of(0, 1)
        for n in (Q_, G_, V_):
            weight_max(n)
        pool.wait_ge(whi_ready, 2 * OUT_ + 1)
        pool.tensor_tensor(w_out[1][:].rearrange("p k d -> p (k d)"), raw_weight(OUT_),
                           w_out[0][:].bitcast(F32).rearrange("p k d -> p (k d)"), ALU.subtract).then_inc(w_out_ready, 1)
        for p in range(UNROLL):
            step(0, p)
            if p == SUM_STEPS - 1:
                pool.wait_ge(msum_ready, 1)
                pool.partition_all_reduce(msum_all[:, 0:MATS], msum[:, 0:MATS], P, bass.bass_isa.ReduceOp.add).then_inc(msum_all_ready, 1)
        with pool.Fori(1, CHUNKS // UNROLL - 1) as i:
            for p in range(UNROLL):
                step(i, p)
        for p in range(UNROLL):
            step(CHUNKS // UNROLL - 1, p, last=True)
        with pool.Fori(0, BLOCKS - 1) as b:
            pool.wait_ge(mv2_ready, b + 1)
            carry(pool)
            pool.tensor_scalar(ln2[:, :, 1:2], ln2[:, :, 1:2], LN_EPS, None, ALU.add).then_inc(vareps2_ready, 1)
            pool.wait_ge(vareps2_ready, b + 1)
            pool.tensor_tensor(rstd2[:], ln2[:, :, 1], minus_half[:, 0:TT], ALU.pow).then_inc(rstd2_ready, 1)
        for tt in range(TT):
            n = BLOCKS + tt
            pool.wait_ge(mv2_ready, n)
            pool.tensor_scalar(ln2[:, tt, 1:2], ln2[:, tt, 1:2], LN_EPS, None, ALU.add).then_inc(vareps2_ready, 1)
            pool.wait_ge(vareps2_ready, n)
            pool.tensor_tensor(rstd2[:, tt:tt + 1], ln2[:, tt, 1:2], minus_half[:, 0:1], ALU.pow).then_inc(rstd2_ready, 1)

    ctx.close()


def kernel(**inputs):
    import concourse.bacc as bacc
    from concourse.bass_utils import run_bass_kernel_spmd

    f = {n: np.asarray(a) for n, a in inputs.items()}

    def contraction_first(w):
        o, i = w.shape
        return w.T.reshape(i // P, P, o).transpose(1, 0, 2)

    w_attn = np.stack([contraction_first(f[f"L0_attn_W{n}"]).reshape(P, KT * D) for n in "kqgvp"])
    mats = [contraction_first(f[f"L0_ffn_W_{n}"]).reshape(P, KT, ET, P).transpose(0, 2, 1, 3).reshape(P, PER_MAT, PIECE)
            for n in ("up", "gate")] + [contraction_first(f["L0_ffn_W_down"]).reshape(P, PER_MAT, PIECE)]
    w_ffn = np.concatenate([m.transpose(1, 0, 2) for m in mats])
    arrays = {
        "x": np.ascontiguousarray(f["L0_attn_x"].reshape(CHUNKS, P, D)),
        "w_attn": np.ascontiguousarray(w_attn),
        "w_ffn": np.ascontiguousarray(w_ffn),
    }
    nc = bacc.Bacc("TRN2", target_bir_lowering=False, num_devices=1)
    args = [nc.dram_tensor(n, a.shape, mybir.dt.from_np(a.dtype), kind="ExternalInput").ap() for n, a in arrays.items()]
    out = nc.dram_tensor("out", (CHUNKS, P, D), F32, kind="ExternalOutput").ap()
    build(nc, *args, out)
    r = run_bass_kernel_spmd(nc, [arrays], core_ids=[0])
    return r.results[0]["out"].reshape(1, TOKENS, D)
```
